# Optimizing a Trainium2 kernel written in Bass

```python
import numpy as np
import jax
import jax.numpy as jnp

def _softmax(x, axis=-1):
    return jax.nn.softmax(x, axis=axis)

def _gelu(x):
    return jax.nn.gelu(x, approximate=True)

def _silu(x):
    return jax.nn.silu(x)

def _sigmoid(x):
    return jax.nn.sigmoid(x)

def _layernorm(x, axis=-1, eps=1e-05):
    m = jnp.mean(x, axis=axis, keepdims=True)
    v = jnp.var(x, axis=axis, keepdims=True)
    return (x - m) / jnp.sqrt(v + eps)

def _scatter_add(tgt, idx, src, axis=0):
    return tgt.at[idx].add(src)

def _segment_sum(src, seg, n):
    return jax.ops.segment_sum(src, seg, n)
kernel_name = 'mk_macaron_d4_jaxref_r8_bc6212'

def setup_inputs(seed: int=0):
    np.random.seed(seed)
    _w = jnp.asarray

    def _L0_attn_setup():
        import jax, jax.numpy as jnp
        import numpy as np
        import math
        B, L, HID, NH = (4, 512, 128, 8)
        DH = HID // NH
        THETA = 10000.0

        def _rope_tables(seq_len, dh):
            half = dh // 2
            inv_freq = 1.0 / THETA ** (jnp.arange(half, dtype=jnp.float32) / half)
            freqs = jnp.arange(seq_len, dtype=jnp.float32)[:, None] * inv_freq[None, :]
            return (jnp.cos(freqs), jnp.sin(freqs))

        def _apply_rope(x, cos, sin):
            half = x.shape[-1] // 2
            x1, x2 = (x[..., :half], x[..., half:2 * half])
            c = cos[None, None]
            s = sin[None, None]
            return jnp.concatenate([x1 * c - x2 * s, x1 * s + x2 * c], axis=-1)
        key = jax.random.key(seed)
        ks = jax.random.split(key, 9)

        def xav(k, sh):
            lim = math.sqrt(6.0 / (sh[0] + sh[1]))
            return jax.random.uniform(k, sh, jnp.float32, -lim, lim)
        return {'x': jax.random.normal(ks[0], (B, L, HID), jnp.float32), 'norm_w': jnp.ones((HID,), jnp.float32), 'Wq': xav(ks[1], (HID, HID)), 'Wk': xav(ks[2], (HID, HID)), 'Wv': xav(ks[3], (HID, HID)), 'Wbeta': xav(ks[4], (NH, HID)), 'bbeta': jnp.full((NH,), 2.0, jnp.float32), 'Wig': xav(ks[5], (NH, HID)), 'big': jnp.zeros((NH,), jnp.float32), 'Wog': xav(ks[6], (NH, HID)), 'bog': jnp.zeros((NH,), jnp.float32), 'Wout': xav(ks[7], (HID, HID)), 'bout': jnp.zeros((HID,), jnp.float32)}
    _L0_attn_in = _L0_attn_setup()

    def _L0_ffn_setup():
        import jax, jax.numpy as jnp
        import numpy as np
        D_MODEL = 128
        key = jax.random.key(seed)
        k_x, k_w, k_a1, k_a2 = jax.random.split(key, 4)
        x = jax.random.normal(k_x, (4, 256, D_MODEL), dtype=jnp.float32)
        weight = jax.random.normal(k_w, (D_MODEL, D_MODEL), dtype=jnp.float32) * 0.02
        aux_weight1 = jax.random.normal(k_a1, (D_MODEL, D_MODEL), dtype=jnp.float32) * 0.02
        aux_weight2 = jax.random.normal(k_a2, (D_MODEL, D_MODEL), dtype=jnp.float32) * 0.02
        bias = jnp.zeros((D_MODEL,), dtype=jnp.float32)
        return {'x': x, 'weight': weight, 'aux_weight1': aux_weight1, 'aux_weight2': aux_weight2, 'bias': bias}
    _L0_ffn_in = _L0_ffn_setup()

    def _L1_attn_setup():
        import math
        import jax, jax.numpy as jnp
        import numpy as np
        NUM_HEADS = 16
        EMBED = 128
        B, T = (2, 256)
        key = jax.random.key(seed)
        k1, k2 = jax.random.split(key)
        x = jax.random.normal(k1, (B, T, EMBED), dtype=jnp.float32)
        bound = 1.0 / math.sqrt(NUM_HEADS * EMBED)
        weight = jax.random.uniform(k2, (NUM_HEADS * EMBED, EMBED), dtype=jnp.float32, minval=-bound, maxval=bound)
        return {'x': x, 'weight': weight}
    _L1_attn_in = _L1_attn_setup()

    def _L1_ffn_setup():
        import jax, jax.numpy as jnp
        import numpy as np
        B, S, H, I, E = (2, 128, 128, 512, 8)
        key = jax.random.key(seed)
        ks = jax.random.split(key, 8)
        s_h = 1.0 / np.sqrt(H)
        s_i = 1.0 / np.sqrt(I)
        return {'x': jax.random.normal(ks[0], (B, S, H), dtype=jnp.float32), 'router_w': jax.random.uniform(ks[1], (H, E), jnp.float32, -s_h, s_h), 'router_b': jax.random.uniform(ks[2], (E,), jnp.float32, -s_h, s_h), 'w1': jax.random.uniform(ks[3], (E, H, I), jnp.float32, -s_h, s_h), 'b1': jax.random.uniform(ks[4], (E, I), jnp.float32, -s_h, s_h), 'w2': jax.random.uniform(ks[5], (E, I, H), jnp.float32, -s_i, s_i), 'b2': jax.random.uniform(ks[6], (E, H), jnp.float32, -s_i, s_i), 'game_emb': jax.random.normal(ks[7], (E, H), dtype=jnp.float32) * 0.02}
    _L1_ffn_in = _L1_ffn_setup()

    def _L2_attn_setup():
        import jax, jax.numpy as jnp
        import numpy as np
        B, S, E, H = (2, 256, 128, 16)
        HD = E // H
        LAMBDA_INIT = 0.8
        EPS = 1e-06
        key = jax.random.key(seed)
        ks = jax.random.split(key, 8)
        return {'x': jax.random.normal(ks[0], (B, S, E), dtype=jnp.float32), 'w_qkv': jax.random.normal(ks[1], (E, 3 * E), dtype=jnp.float32) * E ** (-0.5), 'wo': jax.random.normal(ks[2], (E, E), dtype=jnp.float32) * E ** (-0.5), 'lambda_q1': jax.random.normal(ks[3], (HD,), dtype=jnp.float32) * 0.1, 'lambda_q2': jax.random.normal(ks[4], (HD,), dtype=jnp.float32) * 0.1, 'lambda_k1': jax.random.normal(ks[5], (HD,), dtype=jnp.float32) * 0.1, 'lambda_k2': jax.random.normal(ks[6], (HD,), dtype=jnp.float32) * 0.1, 'norm_w': jnp.ones((H, HD), dtype=jnp.float32)}
    _L2_attn_in = _L2_attn_setup()

    def _L2_ffn_setup():
        import jax, jax.numpy as jnp
        import numpy as np
        B, S, D, H, E = (2, 256, 128, 512, 8)
        key = jax.random.key(seed)
        k0, k1, k2, k3 = jax.random.split(key, 4)
        x = jax.random.normal(k0, (B, S, D), dtype=jnp.float32)
        router_w = jax.random.normal(k1, (E, D), dtype=jnp.float32) * 0.02
        w1 = jax.random.normal(k2, (E, D, H), dtype=jnp.float32) * 0.02
        w2 = jax.random.normal(k3, (E, H, D), dtype=jnp.float32) * 0.02
        return {'x': x, 'router_w': router_w, 'w1': w1, 'w2': w2}
    _L2_ffn_in = _L2_ffn_setup()

    def _L3_attn_setup():
        import jax, jax.numpy as jnp
        import numpy as np
        B, S, E, H = (2, 256, 128, 8)
        DH = E // H
        F = DH // 2
        key = jax.random.key(seed)
        ks = jax.random.split(key, 7)
        sc = E ** (-0.5)
        return {'x': jax.random.normal(ks[0], (B, S, E), dtype=jnp.float32), 'Wq': jax.random.normal(ks[1], (E, E), dtype=jnp.float32) * sc, 'Wk': jax.random.normal(ks[2], (E, E), dtype=jnp.float32) * sc, 'Wv': jax.random.normal(ks[3], (E, E), dtype=jnp.float32) * sc, 'norm_w': jnp.ones((H, DH), dtype=jnp.float32), 'Wo': jax.random.normal(ks[4], (E, E), dtype=jnp.float32) * sc, 'bo': jnp.zeros((E,), dtype=jnp.float32), 'diff_weight': jnp.float32(0.2)}
    _L3_attn_in = _L3_attn_setup()

    def _L3_ffn_setup():
        import jax, jax.numpy as jnp
        import numpy as np
        TOP_K = 2
        key = jax.random.key(seed)
        k_x, k_g, k_w1, k_w2, k_w3 = jax.random.split(key, 5)
        B, S, D, H, E = (2, 64, 128, 64, 8)
        x = jax.random.normal(k_x, (B, S, D), dtype=jnp.float32)
        gate_w = jax.random.normal(k_g, (D, E), dtype=jnp.float32) * D ** (-0.5)
        w1 = jax.random.normal(k_w1, (E, D, H), dtype=jnp.float32) * 0.02
        w2 = jax.random.normal(k_w2, (E, H, D), dtype=jnp.float32) * 0.02
        w3 = jax.random.normal(k_w3, (E, D, H), dtype=jnp.float32) * 0.02
        return {'x': x, 'gate_w': gate_w, 'w1': w1, 'w2': w2, 'w3': w3}
    _L3_ffn_in = _L3_ffn_setup()
    _d = {'L0_attn_x': _L0_attn_in['x'], 'L0_attn_norm_w': _L0_attn_in['norm_w'], 'L0_attn_Wq': _L0_attn_in['Wq'], 'L0_attn_Wk': _L0_attn_in['Wk'], 'L0_attn_Wv': _L0_attn_in['Wv'], 'L0_attn_Wbeta': _L0_attn_in['Wbeta'], 'L0_attn_bbeta': _L0_attn_in['bbeta'], 'L0_attn_Wig': _L0_attn_in['Wig'], 'L0_attn_big': _L0_attn_in['big'], 'L0_attn_Wog': _L0_attn_in['Wog'], 'L0_attn_bog': _L0_attn_in['bog'], 'L0_attn_Wout': _L0_attn_in['Wout'], 'L0_attn_bout': _L0_attn_in['bout'], 'L0_ffn_weight': _L0_ffn_in['weight'], 'L0_ffn_aux_weight1': _L0_ffn_in['aux_weight1'], 'L0_ffn_aux_weight2': _L0_ffn_in['aux_weight2'], 'L0_ffn_bias': _L0_ffn_in['bias'], 'L1_attn_weight': _L1_attn_in['weight'], 'L1_ffn_router_w': _L1_ffn_in['router_w'], 'L1_ffn_router_b': _L1_ffn_in['router_b'], 'L1_ffn_w1': _L1_ffn_in['w1'], 'L1_ffn_b1': _L1_ffn_in['b1'], 'L1_ffn_w2': _L1_ffn_in['w2'], 'L1_ffn_b2': _L1_ffn_in['b2'], 'L1_ffn_game_emb': _L1_ffn_in['game_emb'], 'L2_attn_w_qkv': _L2_attn_in['w_qkv'], 'L2_attn_wo': _L2_attn_in['wo'], 'L2_attn_lambda_q1': _L2_attn_in['lambda_q1'], 'L2_attn_lambda_q2': _L2_attn_in['lambda_q2'], 'L2_attn_lambda_k1': _L2_attn_in['lambda_k1'], 'L2_attn_lambda_k2': _L2_attn_in['lambda_k2'], 'L2_attn_norm_w': _L2_attn_in['norm_w'], 'L2_ffn_router_w': _L2_ffn_in['router_w'], 'L2_ffn_w1': _L2_ffn_in['w1'], 'L2_ffn_w2': _L2_ffn_in['w2'], 'L3_attn_Wq': _L3_attn_in['Wq'], 'L3_attn_Wk': _L3_attn_in['Wk'], 'L3_attn_Wv': _L3_attn_in['Wv'], 'L3_attn_norm_w': _L3_attn_in['norm_w'], 'L3_attn_Wo': _L3_attn_in['Wo'], 'L3_attn_bo': _L3_attn_in['bo'], 'L3_attn_diff_weight': _L3_attn_in['diff_weight'], 'L3_ffn_gate_w': _L3_ffn_in['gate_w'], 'L3_ffn_w1': _L3_ffn_in['w1'], 'L3_ffn_w2': _L3_ffn_in['w2'], 'L3_ffn_w3': _L3_ffn_in['w3']}
    _x0 = _d['L0_attn_x']
    _d['L0_attn_x'] = jax.random.normal(jax.random.fold_in(jax.random.key(seed), 1), (4, 512, 128), dtype=_x0.dtype)
    del _x0
    return _d

def reference(L0_attn_x, L0_attn_norm_w, L0_attn_Wq, L0_attn_Wk, L0_attn_Wv, L0_attn_Wbeta, L0_attn_bbeta, L0_attn_Wig, L0_attn_big, L0_attn_Wog, L0_attn_bog, L0_attn_Wout, L0_attn_bout, L0_ffn_weight, L0_ffn_aux_weight1, L0_ffn_aux_weight2, L0_ffn_bias, L1_attn_weight, L1_ffn_router_w, L1_ffn_router_b, L1_ffn_w1, L1_ffn_b1, L1_ffn_w2, L1_ffn_b2, L1_ffn_game_emb, L2_attn_w_qkv, L2_attn_wo, L2_attn_lambda_q1, L2_attn_lambda_q2, L2_attn_lambda_k1, L2_attn_lambda_k2, L2_attn_norm_w, L2_ffn_router_w, L2_ffn_w1, L2_ffn_w2, L3_attn_Wq, L3_attn_Wk, L3_attn_Wv, L3_attn_norm_w, L3_attn_Wo, L3_attn_bo, L3_attn_diff_weight, L3_ffn_gate_w, L3_ffn_w1, L3_ffn_w2, L3_ffn_w3):

    def _L0_attn_ref(x, norm_w, Wq, Wk, Wv, Wbeta, bbeta, Wig, big, Wog, bog, Wout, bout):
        import jax, jax.numpy as jnp
        import numpy as np
        import math
        B, L, HID, NH = (4, 512, 128, 8)
        DH = HID // NH
        THETA = 10000.0

        def _rope_tables(seq_len, dh):
            half = dh // 2
            inv_freq = 1.0 / THETA ** (jnp.arange(half, dtype=jnp.float32) / half)
            freqs = jnp.arange(seq_len, dtype=jnp.float32)[:, None] * inv_freq[None, :]
            return (jnp.cos(freqs), jnp.sin(freqs))

        def _apply_rope(x, cos, sin):
            half = x.shape[-1] // 2
            x1, x2 = (x[..., :half], x[..., half:2 * half])
            c = cos[None, None]
            s = sin[None, None]
            return jnp.concatenate([x1 * c - x2 * s, x1 * s + x2 * c], axis=-1)
        Bq, Lq, _ = x.shape
        h = x * jax.lax.rsqrt(jnp.mean(x * x, axis=-1, keepdims=True) + 1e-06) * norm_w

        def heads(W):
            return jnp.einsum('bld,ed->ble', h, W).reshape(Bq, Lq, NH, DH).transpose(0, 2, 1, 3)
        q, k, v = (heads(Wq), heads(Wk), heads(Wv))
        cos, sin = _rope_tables(Lq, DH)
        q = _apply_rope(q, cos, sin)
        k = _apply_rope(k, cos, sin)

        def gate(W, b):
            return jax.nn.sigmoid(jnp.einsum('bld,hd->blh', h, W) + b).transpose(0, 2, 1)
        beta, ig, og = (gate(Wbeta, bbeta), gate(Wig, big), gate(Wog, bog))
        scale = 1.0 / math.sqrt(DH)
        qT = q.transpose(2, 0, 1, 3)
        kT = k.transpose(2, 0, 1, 3)
        vT = v.transpose(2, 0, 1, 3)
        fT = beta.transpose(2, 0, 1)
        gT = ig.transpose(2, 0, 1)
        oT = og.transpose(2, 0, 1)
        M0 = jnp.zeros((Bq, NH, DH, DH), x.dtype)

        def step(M, inp):
            q_t, k_t, v_t, f_t, g_t, o_t = inp
            M = M * f_t[..., None, None] + g_t[..., None, None] * scale * (k_t[..., :, None] * v_t[..., None, :])
            y_t = jnp.einsum('bhd,bhde->bhe', q_t, M) * o_t[..., None]
            return (M, y_t)
        _, yT = jax.lax.scan(step, M0, (qT, kT, vT, fT, gT, oT))
        y = yT.transpose(1, 0, 2, 3).reshape(Bq, Lq, HID)
        return jnp.einsum('bld,ed->ble', y, Wout) + bout

    def _L0_ffn_ref(x, weight, aux_weight1, aux_weight2, bias):
        import jax, jax.numpy as jnp
        import numpy as np
        D_MODEL = 128
        h = jnp.einsum('btc,cd->btd', x, weight)
        h = jnp.einsum('btc,cd->btd', h, aux_weight1)
        h = jnp.einsum('btc,cd->btd', h, aux_weight2)
        return jnp.tanh(h + bias)

    def _L1_attn_ref(x, weight):
        import math
        import jax, jax.numpy as jnp
        import numpy as np
        NUM_HEADS = 16
        EMBED = 128
        B, T = (2, 256)
        b, t, c = x.shape
        nh = NUM_HEADS
        hs = c // nh
        y = x.reshape(b, t, nh, hs).transpose(0, 2, 1, 3)
        scores = jnp.einsum('bhtk,bhsk->bhts', y, y) / math.sqrt(hs)
        attn = jax.nn.softmax(scores, axis=-1)
        o = jnp.einsum('bhts,bsc->bhtc', attn, x)
        o = o.transpose(0, 2, 1, 3).reshape(b, t, nh * c)
        return o @ weight

    def _L1_ffn_ref(x, router_w, router_b, w1, b1, w2, b2, game_emb):
        import jax, jax.numpy as jnp
        import numpy as np
        B, S, H, I, E = (2, 128, 128, 512, 8)
        logits = jnp.einsum('bsh,he->bse', x, router_w) + router_b
        expert_idx = jnp.argmax(logits, axis=-1)
        out = jnp.zeros_like(x)
        n_experts = w1.shape[0]
        for e in range(n_experts):
            mask = (expert_idx == e)[..., None]
            sel = x + 0.1 * game_emb[e]
            h = jax.nn.gelu(jnp.einsum('bsh,hi->bsi', sel, w1[e]) + b1[e], approximate=False)
            y = jnp.einsum('bsi,ih->bsh', h, w2[e]) + b2[e]
            out = jnp.where(mask, y, out)
        return out

    def _L2_attn_ref(x, w_qkv, wo, lambda_q1, lambda_q2, lambda_k1, lambda_k2, norm_w):
        import jax, jax.numpy as jnp
        import numpy as np
        B, S, E, H = (2, 256, 128, 16)
        HD = E // H
        LAMBDA_INIT = 0.8
        EPS = 1e-06
        b, s, e = x.shape
        qkv = x @ w_qkv
        q, k, v = jnp.split(qkv, 3, axis=-1)

        def to_heads(t):
            return t.reshape(b, s, H, HD).transpose(0, 2, 1, 3)
        q, k, v = (to_heads(q), to_heads(k), to_heads(v))
        q1, q2 = jnp.split(q, 2, axis=-1)
        k1, k2 = jnp.split(k, 2, axis=-1)
        scale = 1.0 / jnp.sqrt(jnp.asarray(HD, dtype=x.dtype))
        a1 = jax.nn.softmax(jnp.einsum('bhsd,bhtd->bhst', q1, k1) * scale, axis=-1)
        a2 = jax.nn.softmax(jnp.einsum('bhsd,bhtd->bhst', q2, k2) * scale, axis=-1)
        lam = jnp.exp(jnp.dot(lambda_q1, lambda_k1)) - jnp.exp(jnp.dot(lambda_q2, lambda_k2)) + LAMBDA_INIT
        a = a1 - lam * a2
        out = jnp.einsum('bhst,bhtd->bhsd', a, v)
        rms = jnp.sqrt(jnp.mean(out * out, axis=-1, keepdims=True) + EPS)
        out_n = out / rms * norm_w[None, :, None, :] * (1.0 - LAMBDA_INIT)
        out_cat = out_n.reshape(b, H * s, HD)
        out_final = out_cat.transpose(0, 2, 1).reshape(b, s, e)
        return out_final @ wo

    def _L2_ffn_ref(x, router_w, w1, w2):
        import jax, jax.numpy as jnp
        import numpy as np
        B, S, D, H, E = (2, 256, 128, 512, 8)
        b, s, d = x.shape
        e = router_w.shape[0]
        xf = x.reshape(-1, d)
        probs = jax.nn.softmax(xf @ router_w.T, axis=-1)
        topv, topi = jax.lax.top_k(probs, 2)
        topv = topv / (topv.sum(axis=-1, keepdims=True) + 1e-09)
        cw = (jax.nn.one_hot(topi, e, dtype=xf.dtype) * topv[..., None]).sum(axis=1)
        h = jax.nn.gelu(jnp.einsum('td,edh->teh', xf, w1), approximate=False)
        y = jnp.einsum('teh,ehd->ted', h, w2)
        out = jnp.einsum('te,ted->td', cw, y)
        return out.reshape(b, s, d)

    def _L3_attn_ref(x, Wq, Wk, Wv, norm_w, Wo, bo, diff_weight):
        import jax, jax.numpy as jnp
        import numpy as np
        B, S, E, H = (2, 256, 128, 8)
        DH = E // H
        F = DH // 2
        b, s, e = x.shape
        qs = (x @ Wq.T).reshape(b, s, H, 2, F)
        ks_ = (x @ Wk.T).reshape(b, s, H, 2, F)
        vs = (x @ Wv.T).reshape(b, s, H, DH)
        scale = F ** (-0.5)
        scores = jnp.einsum('bqhif,bkhif->ibhqk', qs, ks_) * scale
        atts = jax.nn.softmax(scores, axis=-1)
        att = atts[0] - diff_weight * atts[1]
        o = jnp.einsum('bhqk,bkhe->bqhe', att, vs)
        eps = jnp.finfo(o.dtype).eps
        rms = jax.lax.rsqrt(jnp.mean(o * o, axis=(-2, -1), keepdims=True) + eps)
        normed = (o * rms * norm_w).reshape(b, s, e)
        return (normed @ Wo.T + bo) * (1.0 - diff_weight)

    def _L3_ffn_ref(x, gate_w, w1, w2, w3):
        import jax, jax.numpy as jnp
        import numpy as np
        TOP_K = 2
        B, S, D = x.shape
        E = gate_w.shape[1]
        xf = x.reshape(B * S, D)
        T = B * S
        logits = xf @ gate_w
        scores = jax.nn.softmax(logits, axis=-1)
        top_scores, top_idx = jax.lax.top_k(scores, TOP_K)
        scale = jnp.zeros((T, E), dtype=x.dtype).at[jnp.arange(T)[:, None], top_idx].set(top_scores)
        xs = scale.T[:, :, None] * xf[None, :, :]
        h = jax.nn.silu(jnp.einsum('etd,edh->eth', xs, w1)) * jnp.einsum('etd,edh->eth', xs, w3)
        y = jnp.einsum('eth,ehd->etd', h, w2)
        out = y.sum(axis=0)
        return out.reshape(B, S, D)
    x = L0_attn_x
    x = x + 0.5 * _L0_ffn_ref(_layernorm(x, axis=-1), L0_ffn_weight, L0_ffn_aux_weight1, L0_ffn_aux_weight2, L0_ffn_bias)
    x = x + _L0_attn_ref(_layernorm(x, axis=-1), L0_attn_norm_w, L0_attn_Wq, L0_attn_Wk, L0_attn_Wv, L0_attn_Wbeta, L0_attn_bbeta, L0_attn_Wig, L0_attn_big, L0_attn_Wog, L0_attn_bog, L0_attn_Wout, L0_attn_bout)
    x = x + 0.5 * _L0_ffn_ref(_layernorm(x, axis=-1), L0_ffn_weight, L0_ffn_aux_weight1, L0_ffn_aux_weight2, L0_ffn_bias)
    x = x + 0.5 * _L1_ffn_ref(_layernorm(x, axis=-1), L1_ffn_router_w, L1_ffn_router_b, L1_ffn_w1, L1_ffn_b1, L1_ffn_w2, L1_ffn_b2, L1_ffn_game_emb)
    x = x + _L1_attn_ref(_layernorm(x, axis=-1), L1_attn_weight)
    x = x + 0.5 * _L1_ffn_ref(_layernorm(x, axis=-1), L1_ffn_router_w, L1_ffn_router_b, L1_ffn_w1, L1_ffn_b1, L1_ffn_w2, L1_ffn_b2, L1_ffn_game_emb)
    x = x + 0.5 * _L2_ffn_ref(_layernorm(x, axis=-1), L2_ffn_router_w, L2_ffn_w1, L2_ffn_w2)
    x = x + _L2_attn_ref(_layernorm(x, axis=-1), L2_attn_w_qkv, L2_attn_wo, L2_attn_lambda_q1, L2_attn_lambda_q2, L2_attn_lambda_k1, L2_attn_lambda_k2, L2_attn_norm_w)
    x = x + 0.5 * _L2_ffn_ref(_layernorm(x, axis=-1), L2_ffn_router_w, L2_ffn_w1, L2_ffn_w2)
    x = x + 0.5 * _L3_ffn_ref(_layernorm(x, axis=-1), L3_ffn_gate_w, L3_ffn_w1, L3_ffn_w2, L3_ffn_w3)
    x = x + _L3_attn_ref(_layernorm(x, axis=-1), L3_attn_Wq, L3_attn_Wk, L3_attn_Wv, L3_attn_norm_w, L3_attn_Wo, L3_attn_bo, L3_attn_diff_weight)
    x = x + 0.5 * _L3_ffn_ref(_layernorm(x, axis=-1), L3_ffn_gate_w, L3_ffn_w1, L3_ffn_w2, L3_ffn_w3)
    return x

_drawn_inputs = setup_inputs


def setup_inputs(seed=0):
    import zlib

    import numpy as np

    out = dict(_drawn_inputs(seed))
    spreads = {'L0_attn_norm_w': (1.0, 0.2),
     'L0_attn_bbeta': (2.0, 0.2),
     'L0_attn_big': (0.0, 0.299),
     'L0_attn_bog': (0.0, 0.304),
     'L0_attn_bout': (0.0, 0.1),
     'L0_ffn_bias': (0.0, 0.1),
     'L2_attn_norm_w': (1.0, 0.2),
     'L3_attn_norm_w': (1.0, 0.2),
     'L3_attn_bo': (0.0, 0.1)}
    factors = {'L0_ffn_weight': 2.956,
     'L0_ffn_aux_weight1': 2.916,
     'L0_ffn_aux_weight2': 2.995,
     'L1_ffn_game_emb': 40.246,
     'L2_attn_lambda_q1': 8.0,
     'L2_attn_lambda_q2': 8.0,
     'L2_attn_lambda_k1': 8.0,
     'L2_attn_lambda_k2': 3.473,
     'L3_ffn_gate_w': 8.0,
     'L3_ffn_w1': 8.0,
     'L3_ffn_w2': 8.0,
     'L3_ffn_w3': 8.0}
    for name, (base, spread) in spreads.items():
        noise = np.random.default_rng([zlib.crc32(name.encode()), seed]).standard_normal(out[name].shape)
        drawn = base * np.exp(spread * noise) if base else spread * noise
        out[name] = jnp.asarray(drawn.astype(out[name].dtype))
    for name, factor in factors.items():
        out[name] = (out[name] * factor).astype(out[name].dtype)
    return out
```

```python
from contextlib import ExitStack

import numpy as np

import concourse.bass as bass
from concourse import mybir

F32 = mybir.dt.float32
BF16 = mybir.dt.bfloat16
ALU = mybir.AluOpType
ACT = mybir.ActivationFunctionType
AX = mybir.AxisListType.X

P = 128
B, L, C = 4, 512, 128
NT = B * L // P
TB = L // P
LN_EPS = 1e-5
E = 8
HI = 512
IT = HI // P
H3 = 64
NH0, DH0 = 8, 16
NH1 = 16
SM_SCALE = 8 ** -0.5
NEG = -1e30


class Signal:

    def __init__(self, nc, ctx, name):
        self.sem = ctx.enter_context(nc.semaphore(name))
        self.start = 0

    def at(self, n):
        return n + self.start

    def credit(self, eng):
        eng.sem_inc(self.sem, 1)
        self.start += 1

    def passed(self, n):
        self.start += n


class Chain:

    def __init__(self, eng, signal, base=0):
        self.eng, self.counted, self.base, self.n = eng, signal, base, 0

    def link(self, ins):
        self.n += 1
        ins.then_inc(self.counted.sem, 1)
        self.eng.wait_ge(self.counted.sem, self.counted.at(self.base + self.n))



PARTS = [(0, 0), (0, 1), (1, 0), (0, 2), (2, 0), (1, 1)]


def split_masks(width, dims):
    slots = P // width
    m = np.zeros((P, 4 + 2 * slots), np.float32)
    for s in range(slots):
        for c, (qp, kp) in enumerate(PARTS):
            r = slice(s * width + c * dims, s * width + (c + 1) * dims)
            m[r, 0] = -1.0 if qp else 0.0
            m[r, 1] = 1.0 if qp == 2 else 0.0
            m[r, 2] = -1.0 if kp else 0.0
            m[r, 3] = 1.0 if kp == 2 else 0.0
            m[r, 4 + s] = 1.0
        m[s * width + 6 * dims:s * width + 6 * dims + 2, 4 + slots + s] = 1.0
    return m


def stack_weights(wq, wk, width, dims):
    slots = P // width
    out = np.zeros((C, 8, 2, P), wq.dtype)
    for s in range(8 * slots):
        for c in range(len(PARTS)):
            r = s % slots * width + c * dims
            for side, w in ((0, wq), (1, wk)):
                out[:, s // slots, side, r:r + dims] = w[:, s * dims:(s + 1) * dims]
    return out


def constants():
    r = np.arange(P)
    c = {"ident": np.eye(P, dtype=np.float32)}
    c["upto"] = (r[:, None] <= r[None, :]).astype(np.float32)
    c["after"] = (r[:, None] > r[None, :]).astype(np.float32)
    c["future"] = np.tile(np.where(r[:, None] > r[None, :], np.float32(NEG), np.float32(0)), (1, 4))
    c["headmask"] = (r[:, None] // DH0 == np.arange(NH0)[None, :]).astype(np.float32)
    c["blockmask"] = (r[:, None] // DH0 == r[None, :] // DH0).astype(np.float32)
    half = DH0 // 2
    inv = (1.0 / 10000.0 ** (np.arange(half, dtype=np.float32) / half)).astype(np.float32)
    ang = np.arange(L, dtype=np.float32)[:, None] * inv[None, :]
    cos = np.tile(np.cos(ang), (1, 2 * 2 * NH0)).astype(np.float32)
    sin = np.tile(np.concatenate([-np.sin(ang), np.sin(ang)], axis=1), (1, 2 * NH0)).astype(np.float32)
    c["cos"] = cos.reshape(TB, P, 256).transpose(1, 0, 2).reshape(P, -1)
    c["sin"] = sin.reshape(TB, P, 256).transpose(1, 0, 2).reshape(P, -1)
    c["prefer"] = np.tile((E - np.arange(E)).astype(np.float32), (P, 1))
    c["masks1"] = split_masks(64, 8)
    c["masks2"] = split_masks(32, 4)
    c["masks3"] = split_masks(64, 8)
    sel3 = np.zeros((P, 64), np.float32)
    for j in range(4):
        for d in range(32):
            sel3[32 * j + d, 32 * (j % 2) + d] = 1.0
    c["sel3"] = sel3
    return c



def build(nc, a, out, upto=12, start=0):
    with ExitStack() as ctx:
        k = Kernel(nc, ctx, a, out)
        k.load()
        steps = [lambda: k.ffn0(), lambda: k.gla(), lambda: k.ffn0(),
                 lambda: k.moe(1), lambda: k.attention1(), lambda: k.moe(1),
                 lambda: k.moe(2), lambda: k.attention(2), lambda: k.moe(2),
                 lambda: k.ffn3(), lambda: k.attention(3), lambda: k.ffn3()]
        for s in steps[start:upto]:
            s()
        k.store()


class Kernel:
    def __init__(self, nc, ctx, a, out):
        self.nc, self.ctx, self.a, self.out = nc, ctx, a, out
        self.named = {}
        sb = self.sb
        self.X = sb("X", [P, NT, C])
        self.N = sb("N", [P, NT, C])
        self.nT = sb("nT", [P, NT * P])
        self.ident = sb("ident", [P, P])
        self.identb = sb("identb", [P, P], BF16)
        self.stats = sb("stats", [P, NT, 6])
        self.mv = sb("mv", [P, NT, 2])
        self.rs = sb("rs", [P, 4, NT])
        self.psum = ctx.enter_context(nc.psum_tensor("psum", [P, 8, 512], F32))
        self.banks = [self.psum[:, i, :] for i in range(8)]
        self.cw = sb("cw", [P, NT, E])
        self.rt = sb("rt", [P, 8, NT, E])
        self.prefer = sb("prefer", [P, E])
        self.loads = 0

    def sb(self, name, shape, dt=F32, ctx=None):
        return (ctx or self.ctx).enter_context(self.nc.sbuf_tensor(name, shape, dt))

    def semaphore_of(self, name):
        if name not in self.named:
            self.named[name] = Signal(self.nc, self.ctx, name)
        return self.named[name]

    def load(self):
        nc, a = self.nc, self.a
        loaded = self.semaphore_of("loaded")
        made = self.semaphore_of("made")
        with nc.Block() as block:
            @block.sync
            def _(sp):
                sp.dma_start(self.X[:], a["x"]).then_inc(loaded.sem, 16)
                sp.dma_start(self.ident[:], a["ident"]).then_inc(loaded.sem, 16)
                sp.dma_start(self.prefer[:], a["prefer"]).then_inc(loaded.sem, 16)

            @block.vector
            def _(dve):
                dve.wait_ge(loaded.sem, 48)
                dve.tensor_copy(self.identb[:], self.ident[:]).then_inc(made.sem, 1)
        loaded.passed(48)
        made.passed(1)

    def store(self):
        stored = self.semaphore_of("stored")
        with self.nc.Block() as block:
            @block.sync
            def _(sp):
                sp.dma_start(self.out, self.X[:]).then_inc(stored.sem, 16)
                sp.wait_ge(stored.sem, 16)

    def normalise(self, rms=False, sync=None):
        nc, X, N, nT, rs, mv = self.nc, self.X, self.N, self.nT, self.rs, self.mv
        step = self.semaphore_of("norm_step")
        variance = self.semaphore_of("norm_variance")
        root = self.semaphore_of("norm_root")
        rows = self.semaphore_of("norm_rows")
        turned = self.semaphore_of("norm_turned")
        with nc.Block() as block:
            if sync is not None:
                block.sync(sync)

            @block.vector
            def _(dve):
                ch = Chain(dve, step)
                for t in range(NT):
                    last = dve.bn_stats(self.stats[:, t, :], X[:, t, :])
                ch.link(last)
                for t in range(NT):
                    last = dve.bn_aggr(mv[:, t, :], self.stats[:, t, :])
                ch.link(last)
                dve.tensor_scalar(rs[:, 0, :], mv[:, :, 1], LN_EPS, None, ALU.add).then_inc(variance.sem, 1)
                dve.wait_ge(root.sem, root.at(1))
                ch.link(dve.reciprocal(rs[:, 2, :], rs[:, 1, :]))
                if rms:
                    ch.link(dve.tensor_tensor(rs[:, 3, :], mv[:, :, 1], rs[:, 2, :], ALU.mult))
                    ch.link(dve.tensor_tensor(rs[:, 3, :], rs[:, 3, :], rs[:, 2, :], ALU.mult))
                    dve.tensor_scalar(rs[:, 0, :], rs[:, 3, :], 1e-6, None, ALU.add).then_inc(variance.sem, 1)
                    dve.wait_ge(root.sem, root.at(2))
                    ch.link(dve.reciprocal(rs[:, 3, :], rs[:, 1, :]))
                    ch.link(dve.tensor_tensor(rs[:, 2, :], rs[:, 2, :], rs[:, 3, :], ALU.mult))
                for t in range(NT):
                    ins = dve.tensor_scalar(N[:, t, :], X[:, t, :], mv[:, t, 0:1], rs[:, 2, t:t + 1],
                                            ALU.subtract, ALU.mult)
                    if t % TB == TB - 1:
                        ins.then_inc(rows.sem, 1)

            @block.scalar
            def _(act):
                for n in range(2 if rms else 1):
                    act.wait_ge(variance.sem, variance.at(n + 1))
                    act.activation(rs[:, 1, :], rs[:, 0, :], ACT.Sqrt).then_inc(root.sem, 1)
                for b in range(B):
                    act.wait_ge(turned.sem, turned.at(b + 1))
                    act.activation(nT[:, b * L:(b + 1) * L], self.banks[b][:], ACT.Copy)

            @block.tensor
            def _(pe):
                for b in range(B):
                    pe.wait_ge(rows.sem, rows.at(b + 1))
                    for j in range(TB):
                        last = pe.transpose(self.banks[b][:, j * P:(j + 1) * P], N[:, b * TB + j, :], self.ident[:])
                    last.then_inc(turned.sem, 1)
        step.passed(7 if rms else 3)
        variance.passed(2 if rms else 1)
        root.passed(2 if rms else 1)
        rows.passed(B)
        turned.passed(B)

    def ffn0(self):
        nc, a = self.nc, self.a
        wload = self.semaphore_of("ffn0_weights")
        first = wload.start == 0
        if first:
            self.f0w = self.sb("f0w", [P, 3, P])
            self.f0bias = self.sb("f0bias", [P, P])
            self.f0wt = self.sb("f0wt", [P, P])
            self.f0wc = self.sb("f0wc", [P, P])
            self.f0y = self.sb("f0y", [P, NT, P])

        def load_weights(sp):
            sp.dma_start(self.f0w[:], a["f0w"]).then_inc(wload.sem, 16)
            sp.dma_start(self.f0bias[:], a["f0bias"]).then_inc(wload.sem, 16)

        self.normalise(sync=load_weights if first else None)
        folded = self.semaphore_of("ffn0_folded")
        folds = self.semaphore_of("ffn0_folds")
        lin = self.semaphore_of("ffn0_linear")
        biased = self.semaphore_of("ffn0_biased")
        tanhed = self.semaphore_of("ffn0_tanh")
        w, banks, X, y = self.f0w, self.banks, self.X, self.f0y
        with nc.Block() as block:
            @block.tensor
            def _(pe):
                if first:
                    pe.wait_ge(wload.sem, 32)
                    pe.matmul(banks[4][:, 0:P], w[:, 1, :], w[:, 0, :], start=True, stop=True).then_inc(folded.sem, 1)
                    pe.wait_ge(folds.sem, 1)
                    pe.matmul(banks[5][:, 0:P], self.f0wt[:], w[:, 2, :], start=True, stop=True).then_inc(folded.sem, 1)
                    pe.wait_ge(folds.sem, 2)
                for b in range(B):
                    for j in range(TB):
                        t = b * TB + j
                        last = pe.matmul(banks[b][:, j * P:(j + 1) * P], self.nT[:, t * P:(t + 1) * P],
                                         self.f0wc[:], start=True, stop=True)
                    last.then_inc(lin.sem, 1)

            @block.vector
            def _(dve):
                if first:
                    dve.wait_ge(folded.sem, 1)
                    dve.tensor_copy(self.f0wt[:], banks[4][:, 0:P]).then_inc(folds.sem, 1)
                    dve.wait_ge(folded.sem, 2)
                    dve.tensor_copy(self.f0wc[:], banks[5][:, 0:P]).then_inc(folds.sem, 1)
                for b in range(B):
                    dve.wait_ge(lin.sem, lin.at(b + 1))
                    dve.tensor_tensor(y[:, b * TB:(b + 1) * TB, :], banks[b][:].rearrange("p (t c) -> p t c", t=TB),
                                      self.f0bias[:].unsqueeze(1).broadcast_to([P, TB, P]),
                                      ALU.add).then_inc(biased.sem, 1)
                for b in range(B):
                    dve.wait_ge(tanhed.sem, tanhed.at(b + 1))
                    s = slice(b * TB, (b + 1) * TB)
                    dve.scalar_tensor_tensor(out=X[:, s, :], in0=y[:, s, :], scalar=0.5, in1=X[:, s, :],
                                             op0=ALU.mult, op1=ALU.add)

            @block.scalar
            def _(act):
                for b in range(B):
                    act.wait_ge(biased.sem, biased.at(b + 1))
                    s = slice(b * TB, (b + 1) * TB)
                    act.activation(y[:, s, :], y[:, s, :], ACT.Tanh).then_inc(tanhed.sem, 1)
        if first:
            wload.passed(32)
        for x in (lin, biased, tanhed):
            x.passed(B)

    def gla(self):
        nc, a, X, nT, banks, psum = self.nc, self.a, self.X, self.nT, self.banks, self.psum
        stage = ExitStack()

        def sb(name, shape, dt=F32):
            return self.sb(f"g_{name}", shape, dt, stage)

        W3 = 3 * C
        NG = 3 * NH0
        WA = sb("WA", [P, W3 + NG])
        NWC = sb("NWC", [P, 1])
        GB = sb("GB", [P, NG])
        WO = sb("WO", [P, C])
        BO = sb("BO", [P, C])
        COS = sb("COS", [P, TB * 2 * C])
        SIN = sb("SIN", [P, TB * 2 * C])
        UPTO = sb("UPTO", [P, P])
        AFTER = sb("AFTER", [P, P])
        FUT = sb("FUT", [P, L])
        FUTB = sb("FUTB", [P, L], BF16)
        HM = sb("HM", [P, NH0])
        BM = sb("BM", [P, P])
        ONES = sb("ONES", [P, P])
        MINUS = sb("MINUS", [P, P])
        Z = sb("Z", [P, 4, NT, NG])
        LS = sb("LS", [P, NT, NG])
        SG = sb("SG", [P, NT, 2 * NH0])
        EF = sb("EF", [P, NT, NH0])
        EE = sb("EE", [P, NT, NH0])
        EM = sb("EM", [P, NT, NH0])
        GV = sb("GV", [P, NT, NH0])
        GE = sb("GE", [P, NT, NH0])
        MD = sb("MD", [P, NT])
        HS = sb("HS", [P, 2, P])
        CU = sb("CU", [P, 2, NH0, P])
        T1 = sb("T1", [P, 2 * C])
        T2 = sb("T2", [P, 2 * C])
        QK = sb("QK", [P, 2, 2 * C])
        QKT = sb("QKT", [P, 2, 2 * C])
        QX = sb("QX", [P, 2, NH0, P])
        VG = sb("VG", [P, 2, C])
        VE = sb("VE", [P, 2, C])
        D = sb("D", [P, 2, NH0 * P])
        A = sb("A", [P, 2, NH0 * P])
        Y1 = sb("Y1", [P, C])
        Y2 = sb("Y2", [P, C])
        YO = sb("YO", [P, 2, C])
        YT = sb("YT", [P, 2, C])
        UM = sb("UM", [P, C])
        M = sb("M", [P, B, C])
        loaded = self.semaphore_of("gla_load")
        arrays = [(WA, "gla_w"), (NWC, "gla_nw"), (GB, "gla_gb"), (WO, "gla_wo"), (BO, "gla_bo"), (COS, "cos"),
                  (SIN, "sin"), (UPTO, "upto"), (AFTER, "after"), (FUT, "future"), (HM, "headmask"),
                  (BM, "blockmask")]

        def load(sp):
            for dst, name in arrays:
                sp.dma_start(dst[:], a[name]).then_inc(loaded.sem, 16)
            sp.wait_ge(loaded.sem, 16 * len(arrays))

        self.normalise(rms=True, sync=load)
        names = "weighted gates logs exps sums sumexp step".split()
        loop_names = ("tile cumul expand proj expo decay rot vv qkT qkTc "
                 "sim attn mixed yo state yT yTc outp x rope ystep").split()
        S = {n: self.semaphore_of(f"gla_{n}") for n in names + loop_names}

        with nc.Block() as block:
            @block.gpsimd
            def _(pool):
                for n in loop_names:
                    S[n].credit(pool)

            @block.tensor
            def _(pe):
                pe.wait_ge(S["weighted"].sem, 1)
                for t in range(NT):
                    last = pe.matmul(banks[0][:, t * NG:(t + 1) * NG], nT[:, t * P:(t + 1) * P], WA[:, W3:W3 + NG],
                                     start=True, stop=True)
                last.then_inc(S["gates"].sem, 1)
                pe.wait_ge(S["logs"].sem, 2)
                for n, m in enumerate((UPTO, AFTER, ONES)):
                    last = pe.matmul(banks[1 + n][:, 0:NT * NH0], m[:], LS[:, :, 0:NH0], start=True, stop=True)
                last.then_inc(S["sums"].sem, 1)

            @block.scalar
            def _(act):
                act.wait_ge(S["logs"].sem, 1)
                act.activation(Z[:, 3], Z[:, 1], ACT.Exp, scale=-1.0).then_inc(S["exps"].sem, 1)
                act.wait_ge(S["exps"].sem, 1)
                act.activation(Z[:, 3], Z[:, 3], ACT.Ln, bias=1.0).then_inc(S["exps"].sem, 1)
                act.wait_ge(S["logs"].sem, 2)
                act.activation(SG[:], LS[:, :, NH0:NG], ACT.Exp)
                act.wait_ge(S["sums"].sem, 1)
                for n, e in enumerate((EF, EE, EM)):
                    last = act.activation(e[:], banks[1 + n][:, 0:NT * NH0].rearrange("p (t h) -> p t h", h=NH0),
                                          ACT.Exp)
                last.then_inc(S["sumexp"].sem, 1)

            @block.vector
            def _(dve):
                ch = Chain(dve, S["step"])
                dve.memset(ONES[:], 1.0)
                dve.memset(MINUS[:], -1.0)
                dve.memset(M[:], 0.0)
                dve.tensor_copy(FUTB[:], FUT[:])
                dve.tensor_scalar(WA[:], WA[:], NWC[:, 0:1], None, ALU.mult).then_inc(S["weighted"].sem, 1)
                dve.tensor_tensor(X[:], X[:], BO[:].unsqueeze(1).broadcast_to([P, NT, C]), ALU.add)
                dve.wait_ge(S["gates"].sem, 1)
                z, az, neg = Z[:, 0], Z[:, 1], Z[:, 2]
                ch.link(dve.tensor_tensor(z, banks[0][:, 0:NT * NG].rearrange("p (t g) -> p t g", g=NG),
                                          GB[:].unsqueeze(1).broadcast_to([P, NT, NG]), ALU.add))
                ch.link(dve.tensor_scalar(neg, z, -1.0, None, ALU.mult))
                dve.tensor_tensor(az, z, neg, ALU.max).then_inc(S["logs"].sem, 1)
                ch.link(dve.tensor_scalar(neg, neg, 0.0, None, ALU.max))
                dve.wait_ge(S["exps"].sem, 2)
                dve.scalar_tensor_tensor(out=LS[:], in0=neg, scalar=-1.0, in1=Z[:, 3], op0=ALU.mult,
                                         op1=ALU.subtract).then_inc(S["logs"].sem, 1)
                dve.wait_ge(S["sumexp"].sem, 1)
                ch.link(dve.tensor_scalar(GV[:], SG[:, :, 0:NH0], DH0 ** -0.5, None, ALU.mult))
                dve.tensor_tensor(GE[:], GV[:], EE[:], ALU.mult)
                ch.link(dve.tensor_tensor(Z[:, 0, :, 0:NH0], EM[:], HM[:].unsqueeze(1).broadcast_to([P, NT, NH0]),
                                          ALU.mult))
                dve.tensor_reduce(MD[:], Z[:, 0, :, 0:NH0], AX, ALU.add)

        def tile(ap, c, b):
            return ap[:, bass.ds(c + b * TB, 1)]

        def per_head(ap, c, b, w):
            return tile(ap, c, b).rearrange("p o h -> p (o h)").unsqueeze(2).broadcast_to([P, NH0, w])

        with nc.Block() as block:
            @block.gpsimd
            def _(pool):
                def early(c, b):
                    p = b % 2
                    pool.wait_ge(S["proj"].sem, S["proj"].at(c * B + max(b - 1, 0)))
                    pool.tensor_copy(HS[:, p, :], nT[:, bass.ds(c * P + b * L, P)]).then_inc(S["tile"].sem, 1)
                    pool.wait_ge(S["expo"].sem, S["expo"].at(c * B + max(b - 1, 0)))
                    pool.tensor_tensor(CU[:, p], UPTO[:].unsqueeze(1).broadcast_to([P, NH0, P]),
                                       per_head(LS[:, :, 0:NH0], c, b, P), ALU.mult).then_inc(S["cumul"].sem, 1)

                with pool.Fori(0, TB) as c:
                    early(c, 0)
                    for b in range(B):
                        if b + 1 < B:
                            early(c, b + 1)
                        p = b % 2
                        pool.wait_ge(S["qkTc"].sem, S["qkTc"].at(c * B + b + 1))
                        pool.tensor_tensor(QX[:, p], QKT[:, p, 0:P].unsqueeze(1).broadcast_to([P, NH0, P]),
                                           HM[:].unsqueeze(2).broadcast_to([P, NH0, P]), ALU.mult
                                           ).then_inc(S["expand"].sem, 1)

            @block.tensor
            def _(pe):
                def early(c, b):
                    p = b % 2
                    pe.wait_ge(S["tile"].sem, S["tile"].at(c * B + b + 1))
                    pe.wait_ge(S["vv"].sem, S["vv"].at(c * B + b))
                    pe.matmul(banks[0][:, 0:W3], HS[:, p, :], WA[:, 0:W3], start=True, stop=True
                              ).then_inc(S["proj"].sem, 1)
                    pe.wait_ge(S["cumul"].sem, S["cumul"].at(c * B + b + 1))
                    pe.wait_ge(S["decay"].sem, S["decay"].at(c * B + b))
                    for s in range(2):
                        h4 = CU[:, p, 4 * s:4 * s + 4, :].rearrange("p h t -> p (h t)")
                        pe.matmul(banks[1 + s], ONES[:], h4, start=True, stop=False)
                        for h in range(4):
                            pe.matmul(banks[1 + s][:, h * P:(h + 1) * P], CU[:, p, 4 * s + h, :], MINUS[:],
                                      start=False, stop=False)
                        last = pe.matmul(banks[1 + s], self.identb[:], FUTB[:], start=False, stop=True)
                    last.then_inc(S["expo"].sem, 1)

                with pe.Fori(0, TB) as c:
                    early(c, 0)
                    for b in range(B):
                        n = c * B + b
                        if b + 1 < B:
                            early(c, b + 1)
                        p = b % 2
                        pe.wait_ge(S["rot"].sem, S["rot"].at(n + 1))
                        pe.wait_ge(S["yTc"].sem, S["yTc"].at(n))
                        for s in range(2):
                            last = pe.transpose(banks[3][:, s * P:(s + 1) * P], QK[:, p, s * P:(s + 1) * P], self.ident[:])
                        last.then_inc(S["qkT"].sem, 1)
                        pe.wait_ge(S["expand"].sem, S["expand"].at(n + 1))
                        pe.wait_ge(S["attn"].sem, S["attn"].at(n))
                        for s in range(2):
                            last = pe.matmul(banks[4 + s], QKT[:, p, P:2 * P],
                                             QX[:, p, 4 * s:4 * s + 4, :].rearrange("p h t -> p (h t)"),
                                             start=True, stop=True)
                        last.then_inc(S["sim"].sem, 1)
                        pe.wait_ge(S["state"].sem, S["state"].at(n))
                        pe.matmul(banks[6][:, 2 * C:3 * C], QK[:, p, C:2 * C], VE[:, p, :], start=True, stop=True)
                        pe.matmul(banks[6][:, C:2 * C], QKT[:, p, 0:P], M[:, b, :], start=True, stop=True)
                        pe.wait_ge(S["attn"].sem, S["attn"].at(n + 1))
                        for h in range(NH0):
                            s = slice(h * DH0, (h + 1) * DH0)
                            last = pe.matmul(banks[6][:, s], A[:, p, h * P:(h + 1) * P], VG[:, p, s],
                                             start=True, stop=True)
                        last.then_inc(S["mixed"].sem, 1)
                        pe.wait_ge(S["yo"].sem, S["yo"].at(n + 1))
                        pe.transpose(banks[3][:, 3 * P:4 * P], YO[:, p, :], self.ident[:]).then_inc(S["yT"].sem, 1)
                        pe.wait_ge(S["yTc"].sem, S["yTc"].at(n + 1))
                        pe.wait_ge(S["x"].sem, S["x"].at(n))
                        pe.matmul(banks[7][:, 0:C], YT[:, p, :], WO[:], start=True, stop=True).then_inc(S["outp"].sem, 1)

            @block.scalar
            def _(act):
                act.preload_act_table(ACT.Exp)

                def early(c, b):
                    p = b % 2
                    act.wait_ge(S["expo"].sem, S["expo"].at(c * B + b + 1))
                    act.wait_ge(S["attn"].sem, S["attn"].at(c * B + max(b - 1, 0)))
                    act.activation(D[:, p, :], psum[:, 1:3, :].rearrange("p a n -> p (a n)"), ACT.Exp
                                   ).then_inc(S["decay"].sem, 1)
                with act.Fori(0, TB) as c:
                    early(c, 0)
                    for b in range(B):
                        n = c * B + b
                        if b + 1 < B:
                            early(c, b + 1)
                        p = b % 2
                        act.wait_ge(S["qkT"].sem, S["qkT"].at(n + 1))
                        act.activation(QKT[:, p, :], banks[3][:, 0:2 * P], ACT.Copy).then_inc(S["qkTc"].sem, 1)
                        act.wait_ge(S["yT"].sem, S["yT"].at(n + 1))
                        act.activation(YT[:, p, :], banks[3][:, 3 * P:4 * P], ACT.Copy).then_inc(S["yTc"].sem, 1)

            @block.vector
            def _(dve):
                def early(c, b):
                    p = b % 2
                    r = S["rope"]
                    dve.wait_ge(S["proj"].sem, S["proj"].at(c * B + b + 1))
                    dve.wait_ge(S["rot"].sem, S["rot"].at(c * B + b))
                    dve.wait_ge(S["mixed"].sem, S["mixed"].at(c * B + max(b - 1, 0)))
                    qk = banks[0][:, 0:2 * C].rearrange("p (g i d) -> p g i d", i=2, d=DH0 // 2)
                    t2 = T2[:].rearrange("p (g i d) -> p g i d", i=2, d=DH0 // 2)
                    sin = SIN[:, bass.ds(c * 2 * C, 2 * C)].rearrange("p (g i d) -> p g i d", i=2, d=DH0 // 2)
                    dve.tensor_tensor(T1[:], banks[0][:, 0:2 * C], COS[:, bass.ds(c * 2 * C, 2 * C)], ALU.mult)
                    dve.tensor_tensor(t2[:, :, 0, :], qk[:, :, 1, :], sin[:, :, 0, :], ALU.mult)
                    dve.tensor_tensor(t2[:, :, 1, :], qk[:, :, 0, :], sin[:, :, 1, :], ALU.mult).then_inc(r.sem, 1)
                    v = banks[0][:, 2 * C:W3].rearrange("p (h d) -> p h d", h=NH0)
                    dve.tensor_tensor(VG[:, p].rearrange("p (h d) -> p h d", h=NH0), v, per_head(GV, c, b, DH0), ALU.mult)
                    dve.tensor_tensor(VE[:, p].rearrange("p (h d) -> p h d", h=NH0), v, per_head(GE, c, b, DH0),
                                      ALU.mult).then_inc(S["vv"].sem, 1)
                    dve.wait_ge(r.sem, r.at(c * B + b + 1))
                    dve.tensor_tensor(QK[:, p, :], T1[:], T2[:], ALU.add).then_inc(S["rot"].sem, 1)

                with dve.Fori(0, TB) as c:
                    ch = Chain(dve, S["ystep"], c * 2 * B)
                    early(c, 0)
                    for b in range(B):
                        n = c * B + b
                        if b + 1 < B:
                            early(c, b + 1)
                        p = b % 2
                        dve.wait_ge(S["sim"].sem, S["sim"].at(n + 1))
                        dve.wait_ge(S["decay"].sem, S["decay"].at(n + 1))
                        dve.tensor_tensor(A[:, p, :], psum[:, 4:6, :].rearrange("p a n -> p (a n)"), D[:, p, :],
                                          ALU.mult).then_inc(S["attn"].sem, 1)
                        dve.wait_ge(S["mixed"].sem, S["mixed"].at(n + 1))
                        dve.wait_ge(S["state"].sem, S["state"].at(n))
                        dve.wait_ge(S["yo"].sem, S["yo"].at(n))
                        y1, y2 = Y1[:].rearrange("p (h d) -> p h d", h=NH0), Y2[:].rearrange("p (h d) -> p h d", h=NH0)
                        dve.tensor_tensor(UM[:], banks[6][:, 2 * C:3 * C], BM[:], ALU.mult)
                        ch.link(dve.tensor_tensor(y1, banks[6][:, C:2 * C].rearrange("p (h d) -> p h d", h=NH0),
                                                  per_head(EF, c, b, DH0), ALU.mult))
                        ch.link(dve.tensor_tensor(Y2[:], banks[6][:, 0:C], Y1[:], ALU.add))
                        dve.tensor_tensor(YO[:, p].rearrange("p (h d) -> p h d", h=NH0), y2,
                                          per_head(SG[:, :, NH0:2 * NH0], c, b, DH0), ALU.mult).then_inc(S["yo"].sem, 1)
                        dve.scalar_tensor_tensor(out=M[:, b, :], in0=M[:, b, :],
                                                 scalar=MD[:, bass.ds(c + b * TB, 1)], in1=UM[:],
                                                 op0=ALU.mult, op1=ALU.add).then_inc(S["state"].sem, 1)
                        dve.wait_ge(S["outp"].sem, S["outp"].at(n + 1))
                        xt = tile(X, c, b).rearrange("p o c -> p (o c)")
                        dve.tensor_tensor(xt, banks[7][:, 0:C], xt, ALU.add).then_inc(S["x"].sem, 1)
        stage.close()

    def route(self, kind, weights, bias, counted):
        nc, nT, rt, cw = self.nc, self.nT, self.rt, self.cw
        scored = self.semaphore_of("route_scored")
        step = self.semaphore_of("route_step")
        shifted = self.semaphore_of("route_shifted")
        powered = self.semaphore_of("route_powered")
        steps_seen = []
        s3 = [P, NT, E]

        def over(col):
            return col.unsqueeze(2).broadcast_to(s3)

        with nc.Block() as block:
            @block.gpsimd
            def _(pool):
                for s in counted:
                    if not s.start:
                        s.credit(pool)

            @block.tensor
            def _(pe):
                for t in range(NT):
                    last = pe.matmul(self.banks[0][:, t * E:(t + 1) * E], nT[:, t * P:(t + 1) * P], weights,
                                     start=True, stop=True)
                last.then_inc(scored.sem, 1)

            @block.scalar
            def _(act):
                if kind != 1:
                    act.wait_ge(shifted.sem, shifted.at(1))
                    act.activation(rt[:, 1], rt[:, 0], ACT.Exp).then_inc(powered.sem, 1)

            @block.vector
            def _(dve):
                ch = Chain(dve, step)
                logits = self.banks[0][:, 0:NT * E].rearrange("p (t e) -> p t e", e=E)
                v, e, best, tie, first = rt[:, 0], rt[:, 1], rt[:, 2], rt[:, 3], rt[:, 4]

                def best_of(values, into):
                    col = best[:, :, 0]
                    ch.link(dve.tensor_reduce(col, values, AX, ALU.max))
                    ch.link(dve.tensor_tensor(tie, values, over(col), ALU.is_equal))
                    ch.link(dve.tensor_tensor(tie, tie, self.prefer[:].unsqueeze(1).broadcast_to(s3), ALU.mult))
                    ch.link(dve.tensor_reduce(col, tie, AX, ALU.max))
                    ch.link(dve.tensor_tensor(into, tie, over(col), ALU.is_equal))

                dve.wait_ge(scored.sem, scored.at(1))
                if kind == 1:
                    ch.link(dve.tensor_tensor(v, logits, bias.unsqueeze(1).broadcast_to(s3), ALU.add))
                    best_of(v, first)
                    dve.tensor_scalar(cw[:], first, 0.5, None, ALU.mult)
                else:
                    ch.link(dve.tensor_reduce(best[:, :, 1], logits, AX, ALU.max))
                    dve.tensor_tensor(v, logits, over(best[:, :, 1]), ALU.subtract).then_inc(shifted.sem, 1)
                    dve.wait_ge(powered.sem, powered.at(1))
                    ch.link(dve.tensor_reduce(best[:, :, 1], e, AX, ALU.add))
                    ch.link(dve.reciprocal(best[:, :, 2], best[:, :, 1]))
                    ch.link(dve.tensor_tensor(e, e, over(best[:, :, 2]), ALU.mult))
                    best_of(e, first)
                    ch.link(dve.scalar_tensor_tensor(out=v, in0=first, scalar=-4.0, in1=e, op0=ALU.mult, op1=ALU.add))
                    best_of(v, rt[:, 5])
                    ch.link(dve.tensor_tensor(first, first, rt[:, 5], ALU.add))
                    if kind == 3:
                        dve.tensor_tensor(cw[:], first, e, ALU.mult)
                    else:
                        ch.link(dve.tensor_tensor(first, first, e, ALU.mult))
                        ch.link(dve.tensor_reduce(best[:, :, 3], first, AX, ALU.add))
                        ch.link(dve.tensor_scalar(best[:, :, 4], best[:, :, 3], 1e-9, 2.0, ALU.add, ALU.mult))
                        ch.link(dve.reciprocal(best[:, :, 5], best[:, :, 4]))
                        dve.tensor_tensor(cw[:], first, over(best[:, :, 5]), ALU.mult)
                steps_seen.append(ch.n)
        scored.passed(1)
        step.passed(steps_seen.pop())
        if kind != 1:
            shifted.passed(1)
            powered.passed(1)

    def moe(self, kind):
        nc, a, X, nT, cw, banks = self.nc, self.a, self.X, self.nT, self.cw, self.banks
        rload = self.semaphore_of("moe_small")
        if rload.start == 0:
            self.mw1 = self.sb("mw1", [P, 2, HI])
            self.mw2 = self.sb("mw2", [P, 2, IT, P])
            self.mh = self.sb("mh", [P, 2, IT, L])
            self.my = self.sb("my", [P, 2, TB, P])
            self.router = {kk: self.sb(f"router{kk}", [P, E]) for kk in (1, 2)}
            self.rbias = self.sb("rbias", [P, E])
            self.b1 = self.sb("b1", [P, E, IT])
            self.b1e = self.sb("b1e", [P, 2, IT])
            self.b2 = self.sb("b2", [P, E, P])
            self.game = self.sb("game", [P, E])
        small = rload.start == 0

        def load_small(sp):
            for dst, name in ((self.router[1], "router1"), (self.router[2], "router2"), (self.rbias, "rbias"),
                              (self.b1, "b1"), (self.b2, "b2"), (self.game, "game")):
                sp.dma_start(dst[:], a[name]).then_inc(rload.sem, 16)
            sp.wait_ge(rload.sem, 96)

        self.normalise(sync=load_small if small else None)
        if small:
            rload.passed(96)
        names = ["weights0", "weights1", "up", "gelu", "down", "gamed", "bias", "y", "step"]
        S = {n: self.semaphore_of(f"moe_{n}") for n in names}
        self.route(kind, self.router[kind][:], self.rbias[:] if kind == 1 else None, [S["y"]])
        w1, w2 = a[f"w1_{kind}"], a[f"w2_{kind}"]
        H, one = self.mh, kind == 1
        U = B

        def each_expert(eng, body):
            with eng.Fori(0, E // 2) as i:
                for p in range(2):
                    body(i, p)

        with nc.Block() as block:
            @block.sync
            def _(sp):
                def expert(i, p, e):
                    sp.dma_start(self.mw1[:, p, :], w1[bass.ds(e, 1)].rearrange("e p n -> p (e n)")
                                 ).then_inc(S[f"weights{p}"].sem, 16)
                    sp.dma_start(self.mw2[:, p].rearrange("p a b -> p (a b)"),
                                 w2[bass.ds(e, 1)].rearrange("e p n -> p (e n)")).then_inc(S[f"weights{p}"].sem, 16)
                for p in range(2):
                    expert(0, p, p)
                with sp.Fori(1, E // 2) as i:
                    for p in range(2):
                        sp.wait_ge(S["down"].sem, i * 2 * U + S["down"].at((p - 1) * U))
                        expert(i, p, i * 2 + p)

            @block.tensor
            def _(pe):
                def up(i, p, u):
                    n = (i * 2 + p) * U + u
                    for it in range(IT):
                        if u:
                            pe.wait_ge(S["gelu"].sem, n * IT + S["gelu"].at(it + 1 - IT))
                        pe.matmul(banks[it], self.mw1[:, p, it * P:(it + 1) * P], nT[:, u * L:(u + 1) * L],
                                  start=True, stop=True).then_inc(S["up"].sem, 1)

                def down(i, p, u):
                    n = (i * 2 + p) * U + u
                    if u >= 2:
                        pe.wait_ge(S["y"].sem, n + S["y"].at(-1))
                    for j in range(TB):
                        for it in range(IT):
                            if j == 0:
                                pe.wait_ge(S["gelu"].sem, n * IT + S["gelu"].at(it + 1))
                            last = pe.matmul(banks[4 + u % 2][:, j * P:(j + 1) * P], H[:, u % 2, it, j * P:(j + 1) * P],
                                             self.mw2[:, p, it, :], start=(it == 0), stop=(it == IT - 1))
                    last.then_inc(S["down"].sem, 1)

                def expert(i, p):
                    pe.wait_ge(S[f"weights{p}"].sem, i * 32 + S[f"weights{p}"].at(32))
                    if one:
                        for it in range(IT):
                            last = pe.matmul(banks[6][:, it:it + 1], self.mw1[:, p, it * P:(it + 1) * P],
                                             self.game[:, bass.ds(i * 2 + p, 1)], start=True, stop=True)
                        last.then_inc(S["gamed"].sem, 1)
                    up(i, p, 0)
                    for u in range(U):
                        if u + 1 < U:
                            up(i, p, u + 1)
                        down(i, p, u)

                with pe.Fori(0, E // 2) as i:
                    for p in range(2):
                        pe.wait_ge(S["y"].sem, (i * 2 + p) * U + S["y"].at(0))
                        expert(i, p)

            @block.scalar
            def _(act):
                act.preload_act_table(ACT.Gelu)
                with act.Fori(0, E // 2) as i:
                    for p in range(2):
                        e = i * 2 + p
                        if one:
                            act.wait_ge(S["bias"].sem, e + S["bias"].at(1))
                        for u in range(U):
                            n = e * U + u
                            if u >= 2:
                                act.wait_ge(S["down"].sem, n + S["down"].at(-1))
                            for it in range(IT):
                                act.wait_ge(S["up"].sem, n * IT + S["up"].at(it + 1))
                                act.activation(H[:, u % 2, it, :], banks[it], ACT.Gelu,
                                               bias=self.b1e[:, p, it:it + 1] if one else 0.0
                                               ).then_inc(S["gelu"].sem, 1)

            @block.vector
            def _(dve):
                with dve.Fori(0, E // 2) as i:
                    ch = Chain(dve, S["step"], i * 2 * U)
                    for p in range(2):
                        e = i * 2 + p
                        if one:
                            dve.wait_ge(S["gamed"].sem, e + S["gamed"].at(1))
                            dve.scalar_tensor_tensor(
                                out=self.b1e[:, p, :], in0=banks[6][:, 0:IT], scalar=0.1,
                                in1=self.b1[:, bass.ds(e, 1), :].rearrange("p e n -> p (e n)"),
                                op0=ALU.mult, op1=ALU.add).then_inc(S["bias"].sem, 1)
                        for u in range(U):
                            n = e * U + u
                            dve.wait_ge(S["down"].sem, n + S["down"].at(1))
                            y = banks[4 + u % 2].rearrange("p (t c) -> p t c", t=TB)
                            if one:
                                ch.link(dve.tensor_tensor(self.my[:, u % 2], y,
                                                          self.b2[:, bass.ds(e, 1), :].broadcast_to([P, TB, P]),
                                                          ALU.add))
                                y = self.my[:, u % 2]
                            for j in range(TB):
                                t = u * TB + j
                                last = dve.scalar_tensor_tensor(
                                    out=X[:, t, :], in0=y[:, j, :], scalar=cw[:, t, bass.ds(e, 1)], in1=X[:, t, :],
                                    op0=ALU.mult, op1=ALU.add)
                            last.then_inc(S["y"].sem, 1)
        for p in range(2):
            S[f"weights{p}"].passed(32 * E // 2)
        S["up"].passed(E * U * IT)
        S["gelu"].passed(E * U * IT)
        S["down"].passed(E * U)
        S["y"].passed(E * U)
        if one:
            S["gamed"].passed(E)
            S["bias"].passed(E)
            S["step"].passed(E * U)

    def ffn3(self):
        nc, a, X, nT, cw, banks = self.nc, self.a, self.X, self.nT, self.cw, self.banks
        rload = self.semaphore_of("f3_weights")
        small = rload.start == 0
        if small:
            self.f3w = self.sb("f3w", [P, 2, E * H3])
            self.f3d = self.sb("f3d", [P, IT, P])
            self.f3r = self.sb("f3r", [P, E])
            self.f3n = self.sb("f3n", [P, 2, P])
            self.f3z = self.sb("f3z", [P, 2, 2, E * H3])
            self.f3t = self.sb("f3t", [P, 2, E * H3])
            self.f3h = self.sb("f3h", [P, 2, E * H3])
            self.f3hT = self.sb("f3hT", [P, 2, E * H3])

        def load_small(sp):
            sp.dma_start(self.f3w[:], a["f3w"]).then_inc(rload.sem, 16)
            sp.dma_start(self.f3d[:], a["f3d"]).then_inc(rload.sem, 16)
            sp.dma_start(self.f3r[:], a["f3r"]).then_inc(rload.sem, 16)
            sp.wait_ge(rload.sem, 48)

        self.normalise(sync=load_small if small else None)
        if small:
            rload.passed(48)
        names = ["tile", "proj", "z", "tanh", "h", "turned", "hT", "out", "x", "step"]
        S = {n: self.semaphore_of(f"f3_{n}") for n in names}
        self.route(3, self.f3r[:], None, [S["proj"], S["z"], S["x"]])
        n_, z, th, h, hT = self.f3n, self.f3z, self.f3t, self.f3h, self.f3hT
        M = NT // 2

        def scores(t):
            return cw[:, bass.ds(t, 1), :].rearrange("p o e -> p (o e)").unsqueeze(2).broadcast_to([P, E, H3])

        def v(ap):
            return ap.rearrange("p (e n) -> p e n", e=E)

        with nc.Block() as block:
            @block.gpsimd
            def _(pool):
                with pool.Fori(0, M) as i:
                    for p in range(2):
                        pool.wait_ge(S["proj"].sem, i * 2 + S["proj"].at(0))
                        pool.tensor_copy(n_[:, p, :], nT[:, bass.ds((i * 2 + p) * P, P)]).then_inc(S["tile"].sem, 1)

            @block.tensor
            def _(pe):
                with pe.Fori(0, M) as i:
                    for p in range(2):
                        t = i * 2 + p
                        pe.wait_ge(S["tile"].sem, t + S["tile"].at(1))
                        pe.wait_ge(S["z"].sem, t + S["z"].at(0))
                        for s in range(2):
                            last = pe.matmul(banks[s], n_[:, p, :], self.f3w[:, s, :], start=True, stop=True)
                        last.then_inc(S["proj"].sem, 1)
                        pe.wait_ge(S["h"].sem, t + S["h"].at(1))
                        for it in range(IT):
                            last = pe.transpose(banks[2 + p][:, it * P:(it + 1) * P], h[:, p, it * P:(it + 1) * P], self.ident[:])
                        last.then_inc(S["turned"].sem, 1)
                        pe.wait_ge(S["hT"].sem, t + S["hT"].at(1))
                        pe.wait_ge(S["x"].sem, t + S["x"].at(0))
                        for it in range(IT):
                            last = pe.matmul(banks[4][:, 0:P], hT[:, p, it * P:(it + 1) * P], self.f3d[:, it, :],
                                             start=(it == 0), stop=(it == IT - 1))
                        last.then_inc(S["out"].sem, 1)

            @block.scalar
            def _(act):
                act.preload_act_table(ACT.Tanh)
                with act.Fori(0, M) as i:
                    for p in range(2):
                        t = i * 2 + p
                        act.wait_ge(S["z"].sem, t + S["z"].at(1))
                        act.activation(th[:, p, :], z[:, p, 0, :], ACT.Tanh, scale=0.5).then_inc(S["tanh"].sem, 1)
                        act.wait_ge(S["turned"].sem, t + S["turned"].at(1))
                        act.activation(hT[:, p, :], banks[2 + p], ACT.Copy).then_inc(S["hT"].sem, 1)

            @block.vector
            def _(dve):
                with dve.Fori(0, M) as i:
                    ch = Chain(dve, S["step"], i * 2)
                    for p in range(2):
                        t = i * 2 + p
                        dve.wait_ge(S["proj"].sem, t + S["proj"].at(1))
                        for s in range(2):
                            last = dve.tensor_tensor(v(z[:, p, s, :]), v(banks[s]), scores(t), ALU.mult)
                        last.then_inc(S["z"].sem, 1)
                        dve.wait_ge(S["tanh"].sem, t + S["tanh"].at(1))
                        ch.link(dve.scalar_tensor_tensor(out=th[:, p, :], in0=th[:, p, :], scalar=1.0, in1=z[:, p, 0, :],
                                                         op0=ALU.add, op1=ALU.mult))
                        dve.scalar_tensor_tensor(out=h[:, p, :], in0=th[:, p, :], scalar=0.25, in1=z[:, p, 1, :],
                                                 op0=ALU.mult, op1=ALU.mult).then_inc(S["h"].sem, 1)
                        dve.wait_ge(S["out"].sem, t + S["out"].at(1))
                        xt = X[:, bass.ds(t, 1), :].rearrange("p o c -> p (o c)")
                        dve.tensor_tensor(xt, banks[4][:, 0:P], xt, ALU.add).then_inc(S["x"].sem, 1)
        for x in S.values():
            x.passed(NT)

    def attention(self, kind):
        nc, a, X, N, nT, psum, banks = self.nc, self.a, self.X, self.N, self.nT, self.psum, self.banks
        width, dims = {1: (64, 8), 2: (32, 4), 3: (64, 8)}[kind]
        slots = P // width
        T = slots * TB
        GROUPS = 8
        GC = C // GROUPS
        heads_g = {1: 2, 2: 2, 3: 1}[kind]
        DV = C // (GROUPS * heads_g)
        peaks = kind != 1
        stage = ExitStack()

        def sb(name, shape, dt=F32):
            return self.sb(f"{name}_{kind}", shape, dt, stage)

        WS = sb("WS", [P, GROUPS, 2 * P])
        masks = sb("masks", [P, 4 + 2 * slots])
        wst = sb("wst", [P, 2 * P])
        HIGH = sb("HIGH", [P, 2, L], BF16)
        REST = sb("REST", [P, 2, L])
        LOW = sb("LOW", [P, 2, L], BF16)
        KS = sb("KS", [P, L], BF16)
        QS = sb("QS", [P, B, L], BF16)
        KM = sb("KM", [P, B, slots, L], BF16)
        EX = sb("EX", [P, 2, slots, TB, L])
        aload = self.semaphore_of("at_load")
        aux = [(WS[:].rearrange("p g n -> p (g n)"), f"ws{kind}"), (masks[:], f"masks{kind}")]
        if kind == 1:
            WL = sb("WL", [P, NH1 * P])
            aux.append((WL[:], "wl1"))
            OT = sb("OT", [P, 2, L])
            SUMS = sb("SUMS", [P, 2, slots, TB])
            INV = sb("INV", [P, 2, slots, TB])
        else:
            V = sb("V", [P, NT, C])
            ON = sb("ON", [P, NT, C])
            VST = sb("VST", [P, 2, TB, 2, 32])
            OT = sb("OT", [P, L])
            QM = sb("QM", [P, 2, L], BF16)
            MAXI = sb("MAXI", [P, TB, slots])
            NM = sb("NM", [P, TB, P], BF16)
            INV = sb("INV", [P, TB, slots])
            TMP = sb("TMP", [P, TB * slots, DV])
            WV = sb("WV", [P, C])
            WO = sb("WO", [P, C])
            NW = sb("NW", [P, C])
            MIX = sb("MIX", [P, 4])
            aux += [(WV[:], f"wv{kind}"), (WO[:], f"wo{kind}"), (NW[:], f"nw{kind}")]
            if kind == 2:
                LAM = sb("LAM", [P, 4, 8])
                LSC = sb("LSC", [P, 2, 8])
                LD = sb("LD", [P, 2])
                aux.append((LAM[:].rearrange("p a b -> p (a b)"), "lam"))
                SEL = self.ident
            else:
                BO = sb("BO", [P, C])
                SEL = sb("SEL", [P, 2 * 32])
                aux += [(BO[:], "bo"), (SEL[:], "sel3"), (MIX[:, 0:1], "dw")]
        names = ("proj high rest low stack masked peak reduced negated placed shifted score exp value taken "
                 "gathered joined weights vstage step pstep vproj vready fixed").split()
        S = {n: self.semaphore_of(f"at_{n}") for n in names}

        def load(sp):
            for dst, name in aux:
                sp.dma_start(dst, a[name]).then_inc(aload.sem, 16)
            sp.wait_ge(aload.sem, aload.at(16 * len(aux)))

        self.normalise(sync=load)
        aload.passed(16 * len(aux))

        if kind != 1:
            with nc.Block() as block:
                @block.tensor
                def _(pe):
                    for b in range(B):
                        for j in range(TB):
                            t = b * TB + j
                            last = pe.matmul(banks[b][:, j * P:(j + 1) * P], nT[:, t * P:(t + 1) * P], WV[:],
                                             start=True, stop=True)
                        last.then_inc(S["vproj"].sem, 1)

                @block.scalar
                def _(act):
                    for b in range(B):
                        act.wait_ge(S["vproj"].sem, S["vproj"].at(b + 1))
                        act.activation(V[:, b * TB:(b + 1) * TB, :].rearrange("p t c -> p (t c)"), banks[b], ACT.Copy)
                    if kind == 2:
                        act.wait_ge(S["fixed"].sem, S["fixed"].at(1))
                        act.activation(LD[:], LD[:], ACT.Exp).then_inc(S["vready"].sem, 1)

                @block.vector
                def _(dve):
                    ch = Chain(dve, S["step"])
                    dve.memset(NM[:], 0.0)
                    dve.memset(VST[:], 0.0)
                    if kind == 2:
                        ch.link(dve.tensor_tensor(LSC[:], LAM[:, 0:2], LAM[:, 2:4], ALU.mult))
                        dve.tensor_reduce(LD[:], LSC[:], AX, ALU.add).then_inc(S["fixed"].sem, 1)
                        dve.wait_ge(S["vready"].sem, S["vready"].at(1))
                        ch.link(dve.tensor_tensor(MIX[:, 2:3], LD[:, 1:2], LD[:, 0:1], ALU.subtract))
                        ch.link(dve.tensor_scalar(MIX[:, 0:1], MIX[:, 2:3], -0.8, None, ALU.add))
                    else:
                        ch.link(dve.tensor_scalar(MIX[:, 1:2], MIX[:, 0:1], -1.0, 1.0, ALU.mult, ALU.add))
                        ch.link(dve.tensor_scalar(MIX[:, 0:1], MIX[:, 0:1], -1.0, None, ALU.mult))
                    ch.link(dve.memset(VST[:, :, :, :, DV:DV + 1], 1.0))
            S["vproj"].passed(B)
            if kind == 2:
                S["fixed"].passed(1)
                S["vready"].passed(1)
            S["step"].passed(4 if kind == 2 else 3)

        class Item:

            def __init__(self, G, b, off, first, last):
                self.real = not (first and b + off < 0) and not (last and b + off >= B)
                self.G, self.b = G + (b + off) // B, (b + off) % B
                self.p = self.b % 2
                self.first = first and b + off == 0

            def count(self, name, per, done):
                v = self.G * (B * per) + (self.b * per + done + S[name].start)
                return v

        def drive(eng, step, before=None):
            if before:
                before()
            for b in range(B):
                step(0, b, True, False)
            with eng.Fori(1, GROUPS - 1) as G:
                for b in range(B):
                    step(G, b, False, False)
            for b in range(B):
                step(GROUPS - 1, b, False, True)

        SCORE_BANKS, PEAK_BANKS = (5, 6, 7), (3, 4)

        def last_user(i, ring):
            return (i - ring, False) if i >= ring else (max(k for k in range(T) if k % ring == i % ring), True)

        qmat = QM if peaks else None

        with nc.Block() as block:
            @block.gpsimd
            def _(pool):
                def weights(it):
                    if not it.first:
                        pool.wait_ge(S["proj"].sem, it.count("proj", 2, 0))
                    pool.tensor_copy(wst[:], WS[:, bass.ds(it.G, 1), :].rearrange("p g n -> p (g n)")
                                     ).then_inc(S["weights"].sem, 1)

                def parts(it):
                    for s in range(2):
                        pool.wait_ge(S["rest"].sem, it.count("rest", 2, s + 1))
                        pool.tensor_tensor(LOW[:, s, :], REST[:, s, :],
                                           masks[:, 2 * s + 1:2 * s + 2].broadcast_to([P, L]), ALU.mult
                                           ).then_inc(S["low"].sem, 1)
                        pool.wait_ge(S["low"].sem, it.count("low", 2, s + 1))
                        if s == 1 and not it.first:
                            pool.wait_ge(S["masked"].sem, it.count("masked", 1, 0))
                        dst = QS[:, it.b, :] if s == 0 else KS[:]
                        pool.tensor_tensor(dst, REST[:, s, :], LOW[:, s, :], ALU.subtract).then_inc(S["stack"].sem, 1)

                def values(it):
                    if not (it.first or (it.first_b1)):
                        pool.wait_ge(S["value"].sem, it.count("value", 1, -1))
                    src = V[:, it.b * TB:(it.b + 1) * TB, bass.ds(it.G * GC, GC)]
                    pool.tensor_copy(VST[:, it.p, :, 0:heads_g, 0:DV],
                                     src.rearrange("p t (h d) -> p t h d", h=heads_g)).then_inc(S["vstage"].sem, 1)

                def start():
                    weights(Item(0, 0, 0, True, False))
                    parts(Item(0, 0, 0, True, False))
                    parts(Item(0, 1, 0, True, False))

                def step(G, b, first, last):
                    nxt = Item(G, b, 2, first, last)
                    if kind != 1:
                        it = Item(G, b, 0, first, last)
                        it.first_b1 = first and b <= 1
                        values(it)
                    if nxt.real:
                        if nxt.b == 0:
                            weights(nxt)
                        parts(nxt)
                drive(pool, step, start)

            @block.tensor
            def _(pe):
                def project(it, s):
                    if s == 0 and it.b == 0:
                        pe.wait_ge(S["weights"].sem, it.G + S["weights"].at(1))
                    if s == 1 or not it.first:
                        pe.wait_ge(S["rest"].sem, it.count("rest", 2, s))
                    pe.matmul(banks[0], wst[:, s * P:(s + 1) * P], nT[:, it.b * L:(it.b + 1) * L],
                              start=True, stop=True).then_inc(S["proj"].sem, 1)

                def peak(it, i):
                    j, qt = divmod(i, TB)
                    if i == 0:
                        pe.wait_ge(S["masked"].sem, it.count("masked", 1, 1))
                    tile, before = last_user(i, 2)
                    if not (before and it.first):
                        pe.wait_ge(S["reduced"].sem, it.count("reduced", T, tile + 1 - (T if before else 0)))
                    pe.matmul(banks[PEAK_BANKS[i % 2]], QS[:, it.b, qt * P:(qt + 1) * P], KM[:, it.b, j, :],
                              start=True, stop=True).then_inc(S["peak"].sem, 1)

                def place(it):
                    pe.wait_ge(S["negated"].sem, it.count("negated", 1, 1))
                    if not it.first:
                        pe.wait_ge(S["shifted"].sem, it.count("shifted", 1, 0))
                    for qt in range(TB):
                        last = pe.matmul(banks[1][:, qt * P:(qt + 1) * P], NM[:, qt, :], self.identb[:],
                                         start=True, stop=True)
                    last.then_inc(S["placed"].sem, 1)

                def score(it, i):
                    j, kt = divmod(i, TB)
                    if i == 0:
                        ready = "shifted" if peaks else "masked"
                        pe.wait_ge(S[ready].sem, it.count(ready, 1, 1))
                    tile, before = last_user(i, 3)
                    if not (before and it.first):
                        pe.wait_ge(S["exp"].sem, it.count("exp", T, tile + 1 - (T if before else 0)))
                    q = qmat[:, it.p, :] if peaks else QS[:, it.b, :]
                    pe.matmul(banks[SCORE_BANKS[i % 3]], KM[:, it.b, j, kt * P:(kt + 1) * P], q,
                              start=True, stop=True).then_inc(S["score"].sem, 1)

                def value(it, c):
                    if c == 0:
                        pe.wait_ge(S["exp"].sem, it.count("exp", T, T))
                    if kind == 1:
                        j, kt = divmod(c, TB)
                        if kt == 0 and not it.first:
                            pe.wait_ge(S["taken"].sem, it.count("taken", 2, j - 1))
                        ins = pe.matmul(banks[PEAK_BANKS[j]], N[:, it.b * TB + kt, :], EX[:, it.p, j, kt, :],
                                        start=(kt == 0), stop=(kt == TB - 1))
                        if kt == TB - 1:
                            ins.then_inc(S["value"].sem, 1)
                        return
                    if c == 0:
                        pe.wait_ge(S["vstage"].sem, it.count("vstage", 1, 1))
                        if not it.first:
                            pe.wait_ge(S["joined"].sem, it.count("joined", 1, 0))
                    if kind == 2:
                        for j in range(slots):
                            ins = pe.matmul(banks[2][32 * j:32 * j + 32, :], VST[:, it.p, c, j // 2, :],
                                            EX[:, it.p, j, c, :], start=(c == 0), stop=(c == TB - 1))
                    elif c % 2 == 1:
                        for kt in (c - 1, c):
                            for j in range(slots):
                                at = 32 * (j + 2 * (kt % 2))
                                ins = pe.matmul(banks[2][at:at + 32, :], VST[:, it.p, kt, 0, :],
                                                EX[:, it.p, j, kt, :], start=(kt < 2), stop=(kt >= 2))
                    if c == TB - 1:
                        ins.then_inc(S["value"].sem, 1)

                def gather(it, j=0):
                    if kind == 1:
                        pe.wait_ge(S["taken"].sem, it.count("taken", 2, j + 1))
                        if not it.first:
                            pe.wait_ge(S["joined"].sem, it.count("joined", 2, j - 1))
                        for qt in range(TB):
                            ins = pe.matmul(banks[1 + j][:, qt * P:(qt + 1) * P], OT[:, j, qt * P:(qt + 1) * P],
                                            WL[:, bass.ds((it.G * 2 + j) * P, P)], start=True, stop=True)
                    else:
                        pe.wait_ge(S["taken"].sem, it.count("taken", 1, 1))
                        n = SEL.shape[1]
                        for qt in range(TB):
                            ins = pe.matmul(banks[2][:, qt * n:(qt + 1) * n], OT[:, qt * P:(qt + 1) * P],
                                            SEL[:], start=True, stop=True)
                    ins.then_inc(S["gathered"].sem, 1)

                def start():
                    zero, one = Item(0, 0, 0, True, False), Item(0, 1, 0, True, False)
                    for it in (zero, one):
                        for s in range(2):
                            project(it, s)
                    if peaks:
                        for i in range(T):
                            peak(zero, i)
                        place(zero)

                def step(G, b, first, last):
                    old, now, nxt, new = (Item(G, b, o, first, last) for o in (-1, 0, 1, 2))
                    for i in range(T):
                        if new.real and i in (0, T // 2):
                            project(new, int(i > 0))
                        score(now, i)
                        if peaks and nxt.real:
                            peak(nxt, i)
                        if old.real:
                            if kind == 1:
                                value(old, i)
                                if i == T - 2:
                                    gather(old, 0)
                                if i == T - 1:
                                    gather(old, 1)
                            else:
                                if (i + 1) % (T // 8) == 0 and 1 <= (i + 1) // (T // 8) <= TB:
                                    value(old, (i + 1) // (T // 8) - 1)
                                if i == 3 * T // 4:
                                    gather(old)
                    if peaks and nxt.real:
                        place(nxt)
                drive(pe, step, start)
                end = Item(GROUPS - 1, B - 1, 0, False, True)
                for c in range(T if kind == 1 else TB):
                    value(end, c)
                for j in range(2 if kind == 1 else 1):
                    gather(end, j)

            @block.scalar
            def _(act):
                act.preload_act_table(ACT.Exp)

                def high(it, s):
                    act.wait_ge(S["proj"].sem, it.count("proj", 2, s + 1))
                    act.activation(HIGH[:, s, :], banks[0], ACT.Copy).then_inc(S["high"].sem, 1)

                def exp(it, i):
                    j, kt = divmod(i, TB)
                    if i == 0 and not it.first and not it.second:
                        act.wait_ge(S["value"].sem, it.count("value", 2 if kind == 1 else 1, -2 if kind == 1 else -1))
                        if kind == 1:
                            act.wait_ge(S["fixed"].sem, it.count("fixed", 1, -1))
                    act.wait_ge(S["score"].sem, it.count("score", T, i + 1))
                    act.activation(EX[:, it.p, j, kt, :], banks[SCORE_BANKS[i % 3]], ACT.Exp, scale=SM_SCALE,
                                   accum_out=SUMS[:, it.p, j, kt:kt + 1] if kind == 1 else None
                                   ).then_inc(S["exp"].sem, 1)

                def take(it):
                    act.wait_ge(S["value"].sem, it.count("value", 1, 1))
                    if not it.first:
                        act.wait_ge(S["gathered"].sem, it.count("gathered", 1, 0))
                    act.activation(OT[:], banks[2], ACT.Copy).then_inc(S["taken"].sem, 1)

                def start():
                    for b in range(2):
                        for s in range(2):
                            high(Item(0, b, 0, True, False), s)

                def step(G, b, first, last):
                    old, now, new = (Item(G, b, o, first, last) for o in (-1, 0, 2))
                    now.second = first and b == 1
                    for i in range(T):
                        exp(now, i)
                        if new.real and i in (0, T // 2):
                            high(new, int(i > 0))
                        if kind != 1 and old.real and i == T // 2 + 1:
                            take(old)
                drive(act, step, start)
                if kind != 1:
                    take(Item(GROUPS - 1, B - 1, 0, False, True))

            @block.vector
            def _(dve):
                st, st2 = S["step"], S["pstep"]

                def rest(it, s):
                    dve.wait_ge(S["high"].sem, it.count("high", 2, s + 1))
                    if not it.first:
                        dve.wait_ge(S["stack"].sem, it.count("stack", 2, s - 1))
                    dve.scalar_tensor_tensor(out=REST[:, s, :], in0=HIGH[:, s, :], scalar=masks[:, 2 * s:2 * s + 1],
                                             in1=banks[0], op0=ALU.mult, op1=ALU.add).then_inc(S["rest"].sem, 1)

                def mask(it):
                    dve.wait_ge(S["stack"].sem, it.count("stack", 2, 2))
                    for j in range(slots):
                        ins = dve.tensor_scalar(KM[:, it.b, j, :], KS[:], masks[:, 4 + j:5 + j],
                                                masks[:, 4 + slots + j:5 + slots + j], ALU.mult, ALU.add)
                    ins.then_inc(S["masked"].sem, 1)

                def reduce(it, i):
                    j, qt = divmod(i, TB)
                    dve.wait_ge(S["peak"].sem, it.count("peak", T, i + 1))
                    dve.tensor_reduce(MAXI[:, qt, j:j + 1], banks[PEAK_BANKS[i % 2]], AX, ALU.max
                                      ).then_inc(S["reduced"].sem, 1)

                def negate(it):
                    dve.wait_ge(S["reduced"].sem, it.count("reduced", T, T))
                    if not it.first:
                        dve.wait_ge(S["placed"].sem, it.count("placed", 1, 0))
                    nm = NM[:].rearrange("p t (s w) -> p t s w", s=slots)
                    hi, mid = nm[:, :, :, 6 * dims], nm[:, :, :, 6 * dims + 1]
                    dve.tensor_scalar(hi, MAXI[:], -1.0, None, ALU.mult).then_inc(st.sem, 1)
                    dve.wait_ge(st.sem, it.count("step", 1, 1))
                    dve.scalar_tensor_tensor(out=mid, in0=MAXI[:], scalar=-1.0, in1=hi, op0=ALU.mult,
                                             op1=ALU.subtract).then_inc(S["negated"].sem, 1)

                def shift(it):
                    dve.wait_ge(S["placed"].sem, it.count("placed", 1, 1))
                    dve.tensor_tensor(QM[:, it.p, :], banks[1], QS[:, it.b, :], ALU.add).then_inc(S["shifted"].sem, 1)

                def take(it, j):
                    dve.wait_ge(S["value"].sem, it.count("value", 2, j + 1))
                    if not it.first:
                        dve.wait_ge(S["gathered"].sem, it.count("gathered", 2, j - 1))
                    dve.tensor_copy(OT[:, j, :], banks[PEAK_BANKS[j]]).then_inc(S["taken"].sem, 1)

                def invert(it):
                    dve.wait_ge(S["exp"].sem, it.count("exp", T, T))
                    dve.reciprocal(INV[:, it.p], SUMS[:, it.p]).then_inc(S["fixed"].sem, 1)

                def join1(it, j):
                    dve.wait_ge(S["gathered"].sem, it.count("gathered", 2, j + 1))
                    dve.wait_ge(S["fixed"].sem, it.count("fixed", 1, 1))
                    if j == 1:
                        dve.wait_ge(S["joined"].sem, it.count("joined", 2, 1))
                    for qt in range(TB):
                        t = it.b * TB + qt
                        ins = dve.scalar_tensor_tensor(out=X[:, t, :], in0=banks[1 + j][:, qt * P:(qt + 1) * P],
                                                       scalar=INV[:, it.p, j, qt:qt + 1], in1=X[:, t, :],
                                                       op0=ALU.mult, op1=ALU.add)
                    ins.then_inc(S["joined"].sem, 1)

                def join(it, base):
                    n = SEL.shape[1] // slots if kind == 2 else 32
                    O = banks[2][:, 0:TB * slots * n].rearrange("p (t s w) -> p t s w", t=TB, s=slots)
                    dve.wait_ge(S["gathered"].sem, it.count("gathered", 1, 1))
                    dve.reciprocal(INV[:], O[:, :, :, DV]).then_inc(st2.sem, 1)
                    dve.wait_ge(st2.sem, base(1))
                    odd = INV[:].rearrange("p t (h i) -> p t h i", i=2)[:, :, :, 1]
                    dve.tensor_scalar(odd, odd, MIX[:, 0:1], None, ALU.mult).then_inc(st2.sem, 1)
                    dve.wait_ge(st2.sem, base(2))
                    dve.tensor_tensor(TMP[:], O.rearrange("p t s w -> p (t s) w")[:, :, 0:DV],
                                      INV[:].rearrange("p t s -> p (t s)").unsqueeze(2).broadcast_to([P, TB * slots, DV]),
                                      ALU.mult).then_inc(st2.sem, 1)
                    dve.wait_ge(st2.sem, base(3))
                    both = TMP[:].rearrange("p (t h i) d -> p t h i d", t=TB, i=2)
                    out = ON[:, it.b * TB:(it.b + 1) * TB, bass.ds(it.G * GC, GC)]
                    dve.tensor_tensor(out.rearrange("p t (h d) -> p t h d", h=heads_g), both[:, :, :, 0, :],
                                      both[:, :, :, 1, :], ALU.add).then_inc(S["joined"].sem, 1)

                def start():
                    zero, one = Item(0, 0, 0, True, False), Item(0, 1, 0, True, False)
                    for it in (zero, one):
                        for s in range(2):
                            rest(it, s)
                        mask(it)
                    if peaks:
                        for i in range(T):
                            reduce(zero, i)
                        negate(zero)
                        shift(zero)

                def step(G, b, first, last):
                    old, now, nxt, new = (Item(G, b, o, first, last) for o in (-1, 0, 1, 2))
                    for i in range(T):
                        if peaks and nxt.real:
                            reduce(nxt, i)
                        if new.real and i in (1, T // 2 + 1):
                            rest(new, int(i > 1))
                        if kind == 1 and old.real:
                            if i == TB:
                                take(old, 0)
                    if kind == 1:
                        if old.real:
                            take(old, 1)
                            join1(old, 0)
                            join1(old, 1)
                        invert(now)
                        if new.real:
                            mask(new)
                        return
                    if nxt.real:
                        negate(nxt)
                    if new.real:
                        mask(new)
                    if nxt.real:
                        shift(nxt)
                    if old.real:
                        join(old, lambda k: old.count("pstep", 3, k))
                drive(dve, step, start)
                end = Item(GROUPS - 1, B - 1, 0, False, True)
                if kind == 1:
                    for j in range(2):
                        take(end, j)
                    for j in range(2):
                        join1(end, j)
                else:
                    join(end, lambda k: end.count("pstep", 3, k))

        items = GROUPS * B
        for n in ("proj", "high", "rest", "low", "stack"):
            S[n].passed(2 * items)
        S["masked"].passed(items)
        S["weights"].passed(GROUPS)
        S["score"].passed(T * items)
        S["exp"].passed(T * items)
        two = 2 if kind == 1 else 1
        for n in ("value", "taken", "gathered", "joined"):
            S[n].passed(two * items)
        if kind == 1:
            S["fixed"].passed(items)
        else:
            for n in ("peak", "reduced"):
                S[n].passed(T * items)
            for n in ("negated", "placed", "shifted", "vstage", "step"):
                S[n].passed(items)
            S["pstep"].passed(3 * items)
            self.attention_out(kind, S, ON, NW, WO, MIX, BO if kind == 3 else None, EX)
        stage.close()

    def attention1(self):
        self.attention(1)

    def attention_out(self, kind, S, ON, NW, WO, MIX, BO, EX):
        nc, X, banks = self.nc, self.X, self.banks
        step, sqrt_in, sqrt_out = S["step"], S["negated"], S["placed"]
        ready, proj, turned, taken = S["shifted"], S["gathered"], S["value"], S["taken"]
        flat = EX[:].rearrange("p a s t l -> p (a s t l)")
        SQ = flat[:, 0:NT * C].rearrange("p (t c) -> p t c", t=NT)
        ONT = flat[:, NT * C:2 * NT * C]
        G = 16 if kind == 2 else 1
        W = C // G
        RM = flat[:, 2 * NT * C:2 * NT * C + 3 * NT * 16].rearrange("p (a n) -> p a n", a=3)[:, :, 0:NT * G]
        eps = 1e-6 if kind == 2 else float(np.finfo(np.float32).eps)
        with nc.Block() as block:
            @block.vector
            def _(dve):
                ch = Chain(dve, step)
                on = ON[:].rearrange("p t c -> p (t c)")
                grouped = ON[:].rearrange("p t (g w) -> p (t g) w", g=G)
                ch.link(dve.tensor_tensor(SQ, ON[:], ON[:], ALU.mult))
                ch.link(dve.tensor_reduce(RM[:, 0, :], SQ.rearrange("p t (g w) -> p (t g) w", g=G), AX, ALU.add))
                dve.tensor_scalar(RM[:, 1, :], RM[:, 0, :], 1.0 / W, eps, ALU.mult, ALU.add).then_inc(sqrt_in.sem, 1)
                dve.wait_ge(sqrt_out.sem, sqrt_out.at(1))
                ch.link(dve.reciprocal(RM[:, 1, :], RM[:, 2, :]))
                ch.link(dve.tensor_tensor(grouped, grouped, RM[:, 1, :].unsqueeze(2).broadcast_to([P, NT * G, W]),
                                          ALU.mult))
                if kind == 2:
                    for b in range(B):
                        for t in range(TB):
                            ins = dve.scalar_tensor_tensor(
                                out=ONT[:, b * L:(b + 1) * L].rearrange("p (d h t) -> p t h d", d=8, t=TB)[:, t],
                                in0=ON[:, b * TB + t, :].rearrange("p (h d) -> p h d", d=8), scalar=0.2,
                                in1=NW[:].rearrange("p (h d) -> p h d", d=8), op0=ALU.mult, op1=ALU.mult)
                        ins.then_inc(ready.sem, 1)
                else:
                    for b in range(B):
                        s = slice(b * TB, (b + 1) * TB)
                        dve.tensor_tensor(ON[:, s, :], ON[:, s, :], NW[:].unsqueeze(1).broadcast_to([P, TB, C]),
                                          ALU.mult).then_inc(ready.sem, 1)
                for b in range(B):
                    dve.wait_ge(proj.sem, proj.at(b + 1))
                    s = slice(b * TB, (b + 1) * TB)
                    y = banks[4 + b].rearrange("p (t c) -> p t c", t=TB)
                    if kind == 3:
                        ch.link(dve.tensor_tensor(SQ[:, s, :], y, BO[:].unsqueeze(1).broadcast_to([P, TB, C]), ALU.add))
                        dve.scalar_tensor_tensor(out=X[:, s, :], in0=SQ[:, s, :], scalar=MIX[:, 1:2], in1=X[:, s, :],
                                                 op0=ALU.mult, op1=ALU.add)
                    else:
                        dve.tensor_tensor(X[:, s, :], y, X[:, s, :], ALU.add)

            @block.scalar
            def _(act):
                act.wait_ge(sqrt_in.sem, sqrt_in.at(1))
                act.activation(RM[:, 2, :], RM[:, 1, :], ACT.Sqrt).then_inc(sqrt_out.sem, 1)
                if kind == 3:
                    for b in range(B):
                        act.wait_ge(turned.sem, turned.at(b + 1))
                        act.activation(ONT[:, b * L:(b + 1) * L], banks[b], ACT.Copy).then_inc(taken.sem, 1)

            @block.tensor
            def _(pe):
                if kind == 3:
                    for b in range(B):
                        pe.wait_ge(ready.sem, ready.at(b + 1))
                        for j in range(TB):
                            last = pe.transpose(banks[b][:, j * P:(j + 1) * P], ON[:, b * TB + j, :], self.ident[:])
                        last.then_inc(turned.sem, 1)
                for b in range(B):
                    src = taken if kind == 3 else ready
                    pe.wait_ge(src.sem, src.at(b + 1))
                    for j in range(TB):
                        last = pe.matmul(banks[4 + b][:, j * P:(j + 1) * P], ONT[:, b * L + j * P:b * L + (j + 1) * P],
                                         WO[:], start=True, stop=True)
                    last.then_inc(proj.sem, 1)
        step.passed(8 if kind == 3 else 4)
        sqrt_in.passed(1)
        sqrt_out.passed(1)
        ready.passed(B)
        proj.passed(B)
        if kind == 3:
            turned.passed(B)
            taken.passed(B)



def token_tiles(x):
    return np.ascontiguousarray(np.asarray(x).reshape(NT, P, C).transpose(1, 0, 2))


def everywhere(v):
    return np.ascontiguousarray(np.broadcast_to(np.asarray(v).reshape(1, -1), (P, np.asarray(v).size)))


def layout(i):
    i = {k: np.asarray(v) for k, v in i.items()}
    a = {"x": token_tiles(i["L0_attn_x"])}
    a |= constants()
    a["f0w"] = np.stack([i["L0_ffn_weight"].T, i["L0_ffn_aux_weight1"], i["L0_ffn_aux_weight2"]], axis=1)
    a["f0bias"] = everywhere(i["L0_ffn_bias"])
    a["router1"] = i["L1_ffn_router_w"]
    a["router2"] = i["L2_ffn_router_w"].T
    a["rbias"] = everywhere(i["L1_ffn_router_b"])
    a["b1"] = i["L1_ffn_b1"].reshape(E, IT, P).transpose(2, 0, 1)
    a["b2"] = everywhere(i["L1_ffn_b2"]).reshape(P, E, P)
    a["game"] = i["L1_ffn_game_emb"].T
    for n in (1, 2):
        a[f"w1_{n}"] = i[f"L{n}_ffn_w1"]
        a[f"w2_{n}"] = i[f"L{n}_ffn_w2"].reshape(E, IT, P, C).transpose(0, 2, 1, 3).reshape(E, P, IT * C)
    w1, w3 = (i[f"L3_ffn_{w}"].transpose(1, 0, 2).reshape(C, E * H3) for w in ("w1", "w3"))
    a["f3w"] = np.stack([w1, w3], axis=1)
    a["f3d"] = i["L3_ffn_w2"].reshape(IT, P, C).transpose(1, 0, 2)
    a["f3r"] = i["L3_ffn_gate_w"]
    eye = np.eye(C, dtype=np.float32)
    a["ws1"] = stack_weights(eye, eye, 64, 8).reshape(C, -1)
    a["wl1"] = i["L1_attn_weight"].reshape(NH1, C, C).transpose(1, 0, 2).reshape(C, NH1 * C)
    qkv = i["L2_attn_w_qkv"]
    a["ws2"] = stack_weights(qkv[:, 0:C], qkv[:, C:2 * C], 32, 4).reshape(C, -1)
    a["ws3"] = stack_weights(i["L3_attn_Wq"].T, i["L3_attn_Wk"].T, 64, 8).reshape(C, -1)
    a["wv2"], a["wv3"] = qkv[:, 2 * C:], i["L3_attn_Wv"].T
    a["wo2"], a["wo3"] = i["L2_attn_wo"], i["L3_attn_Wo"].T
    a["nw2"], a["nw3"] = everywhere(i["L2_attn_norm_w"]), everywhere(i["L3_attn_norm_w"])
    a["lam"] = everywhere(np.concatenate([i[f"L2_attn_lambda_{n}"] for n in ("q1", "q2", "k1", "k2")]))
    a["bo"] = everywhere(i["L3_attn_bo"])
    a["dw"] = everywhere(i["L3_attn_diff_weight"])
    a["gla_w"] = np.concatenate([i[f"L0_attn_{n}"] for n in ("Wq", "Wk", "Wv", "Wbeta", "Wig", "Wog")]).T
    a["gla_nw"] = i["L0_attn_norm_w"].reshape(C, 1)
    a["gla_gb"] = everywhere(np.concatenate([i[f"L0_attn_{n}"] for n in ("bbeta", "big", "bog")]))
    a["gla_wo"], a["gla_bo"] = i["L0_attn_Wout"].T, everywhere(i["L0_attn_bout"])
    return {k: np.ascontiguousarray(v) for k, v in a.items()}



def kernel(**inputs):
    import concourse.bacc as bacc
    from concourse.bass_utils import run_bass_kernel_spmd

    nc = bacc.Bacc("TRN2", target_bir_lowering=False, num_devices=1)
    arrays = {f"in_{name}_dram": x for name, x in layout(inputs).items()}
    aps = {name[3:-5]: nc.dram_tensor(name, x.shape, mybir.dt.from_np(x.dtype), kind="ExternalInput").ap()
           for name, x in arrays.items()}
    out = nc.dram_tensor("out_0_dram", (P, NT, C), F32, kind="ExternalOutput").ap()
    build(nc, aps, out)
    r = run_bass_kernel_spmd(nc, [arrays], core_ids=[0])
    return np.ascontiguousarray(r.results[0]["out_0_dram"].transpose(1, 0, 2)).reshape(B, L, C)
```

```python
from contextlib import ExitStack

import numpy as np

import concourse.bass as bass
from concourse import mybir

F32 = mybir.dt.float32
BF16 = mybir.dt.bfloat16
ALU = mybir.AluOpType
ACT = mybir.ActivationFunctionType
AX = mybir.AxisListType.X

P = 128
B, L, C = 4, 512, 128
NT = B * L // P
TB = L // P
LN_EPS = 1e-5
E = 8
HI = 512
IT = HI // P
H3 = 64
NH0, DH0 = 8, 16
NH1 = 16
SM_SCALE = 8 ** -0.5
NEG = -1e30


class Signal:

    def __init__(self, nc, ctx, name):
        self.sem = ctx.enter_context(nc.semaphore(name))
        self.start = 0

    def at(self, n):
        return n + self.start

    def credit(self, eng):
        eng.sem_inc(self.sem, 1)
        self.start += 1

    def passed(self, n):
        self.start += n


class Chain:

    def __init__(self, eng, signal, base=0):
        self.eng, self.counted, self.base, self.n = eng, signal, base, 0

    def link(self, ins):
        self.n += 1
        ins.then_inc(self.counted.sem, 1)
        self.eng.wait_ge(self.counted.sem, self.counted.at(self.base + self.n))



PARTS = [(0, 0), (0, 1), (1, 0), (0, 2), (2, 0), (1, 1)]


def split_masks(width, dims):
    slots = P // width
    m = np.zeros((P, 4 + 2 * slots), np.float32)
    for s in range(slots):
        for c, (qp, kp) in enumerate(PARTS):
            r = slice(s * width + c * dims, s * width + (c + 1) * dims)
            m[r, 0] = -1.0 if qp else 0.0
            m[r, 1] = 1.0 if qp == 2 else 0.0
            m[r, 2] = -1.0 if kp else 0.0
            m[r, 3] = 1.0 if kp == 2 else 0.0
            m[r, 4 + s] = 1.0
        m[s * width + 6 * dims:s * width + 6 * dims + 2, 4 + slots + s] = 1.0
    return m


def stack_weights(wq, wk, width, dims):
    slots = P // width
    out = np.zeros((C, 8, 2, P), wq.dtype)
    for s in range(8 * slots):
        for c in range(len(PARTS)):
            r = s % slots * width + c * dims
            for side, w in ((0, wq), (1, wk)):
                out[:, s // slots, side, r:r + dims] = w[:, s * dims:(s + 1) * dims]
    return out.transpose(1, 0, 2, 3).reshape(8, C, 2 * P)


def constants():
    r = np.arange(P)
    c = {"ident": np.eye(P, dtype=np.float32)}
    c["upto"] = (r[:, None] <= r[None, :]).astype(np.float32)
    c["after"] = (r[:, None] > r[None, :]).astype(np.float32)
    c["future"] = np.tile(np.where(r[:, None] > r[None, :], np.float32(NEG), np.float32(0)), (1, 4))
    c["headmask"] = (r[:, None] // DH0 == np.arange(NH0)[None, :]).astype(np.float32)
    c["blockmask"] = (r[:, None] // DH0 == r[None, :] // DH0).astype(np.float32)
    half = DH0 // 2
    inv = (1.0 / 10000.0 ** (np.arange(half, dtype=np.float32) / half)).astype(np.float32)
    ang = np.arange(L, dtype=np.float32)[:, None] * inv[None, :]
    cos = np.tile(np.cos(ang), (1, 2 * 2 * NH0)).astype(np.float32)
    sin = np.tile(np.concatenate([-np.sin(ang), np.sin(ang)], axis=1), (1, 2 * NH0)).astype(np.float32)
    c["cos"] = cos.reshape(TB, P, 256).transpose(1, 0, 2).reshape(P, -1)
    c["sin"] = sin.reshape(TB, P, 256).transpose(1, 0, 2).reshape(P, -1)
    c["prefer"] = np.tile((E - np.arange(E)).astype(np.float32), (P, 1))
    c["masks1"] = split_masks(64, 8)
    c["masks2"] = split_masks(32, 4)
    c["masks3"] = split_masks(64, 8)
    sel3 = np.zeros((P, 64), np.float32)
    for j in range(4):
        for d in range(32):
            sel3[32 * j + d, 32 * (j % 2) + d] = 1.0
    c["sel3"] = sel3
    return c



def build(nc, a, out, upto=12, start=0):
    with ExitStack() as ctx:
        k = Kernel(nc, ctx, a, out)
        k.load()
        steps = [lambda: k.ffn0(), lambda: k.gla(), lambda: k.ffn0(),
                 lambda: k.moe(1), lambda: k.attention1(), lambda: k.moe(1),
                 lambda: k.moe(2), lambda: k.attention(2), lambda: k.moe(2),
                 lambda: k.ffn3(), lambda: k.attention(3), lambda: k.ffn3()]
        for s in steps[start:upto]:
            s()
        k.store()


class Kernel:
    def __init__(self, nc, ctx, a, out):
        self.nc, self.ctx, self.a, self.out = nc, ctx, a, out
        self.named = {}
        sb = self.sb
        self.X = sb("X", [P, NT, C])
        self.N = sb("N", [P, NT, C])
        self.nT = sb("nT", [P, NT * P])
        self.ident = sb("ident", [P, P])
        self.identb = sb("identb", [P, P], BF16)
        self.stats = sb("stats", [P, NT, 6])
        self.mv = sb("mv", [P, NT, 2])
        self.rs = sb("rs", [P, 4, NT])
        self.psum = ctx.enter_context(nc.psum_tensor("psum", [P, 8, 512], F32))
        self.banks = [self.psum[:, i, :] for i in range(8)]
        self.cw = sb("cw", [P, NT, E])
        self.rt = sb("rt", [P, 8, NT, E])
        self.prefer = sb("prefer", [P, E])
        self.loads = 0

    def sb(self, name, shape, dt=F32, ctx=None):
        return (ctx or self.ctx).enter_context(self.nc.sbuf_tensor(name, shape, dt))

    def semaphore_of(self, name):
        if name not in self.named:
            self.named[name] = Signal(self.nc, self.ctx, name)
        return self.named[name]

    def load(self):
        nc, a = self.nc, self.a
        loaded = self.semaphore_of("loaded")
        made = self.semaphore_of("made")
        with nc.Block() as block:
            @block.sync
            def _(sp):
                sp.dma_start(self.X[:], a["x"]).then_inc(loaded.sem, 16)
                sp.dma_start(self.ident[:], a["ident"]).then_inc(loaded.sem, 16)
                sp.dma_start(self.prefer[:], a["prefer"]).then_inc(loaded.sem, 16)

            @block.vector
            def _(dve):
                dve.wait_ge(loaded.sem, 48)
                dve.tensor_copy(self.identb[:], self.ident[:]).then_inc(made.sem, 1)
        loaded.passed(48)
        made.passed(1)

    def store(self):
        stored = self.semaphore_of("stored")
        with self.nc.Block() as block:
            @block.sync
            def _(sp):
                sp.dma_start(self.out, self.X[:]).then_inc(stored.sem, 16)
                sp.wait_ge(stored.sem, 16)

    def normalise(self, rms=False, sync=None):
        nc, X, N, nT, rs, mv = self.nc, self.X, self.N, self.nT, self.rs, self.mv
        step = self.semaphore_of("norm_step")
        variance = self.semaphore_of("norm_variance")
        root = self.semaphore_of("norm_root")
        rows = self.semaphore_of("norm_rows")
        turned = self.semaphore_of("norm_turned")
        with nc.Block() as block:
            if sync is not None:
                block.sync(sync)

            @block.vector
            def _(dve):
                ch = Chain(dve, step)
                for t in range(NT):
                    last = dve.bn_stats(self.stats[:, t, :], X[:, t, :])
                ch.link(last)
                for t in range(NT):
                    last = dve.bn_aggr(mv[:, t, :], self.stats[:, t, :])
                ch.link(last)
                dve.tensor_scalar(rs[:, 0, :], mv[:, :, 1], LN_EPS, None, ALU.add).then_inc(variance.sem, 1)
                dve.wait_ge(root.sem, root.at(1))
                ch.link(dve.reciprocal(rs[:, 2, :], rs[:, 1, :]))
                if rms:
                    ch.link(dve.tensor_tensor(rs[:, 3, :], mv[:, :, 1], rs[:, 2, :], ALU.mult))
                    ch.link(dve.tensor_tensor(rs[:, 3, :], rs[:, 3, :], rs[:, 2, :], ALU.mult))
                    dve.tensor_scalar(rs[:, 0, :], rs[:, 3, :], 1e-6, None, ALU.add).then_inc(variance.sem, 1)
                    dve.wait_ge(root.sem, root.at(2))
                    ch.link(dve.reciprocal(rs[:, 3, :], rs[:, 1, :]))
                    ch.link(dve.tensor_tensor(rs[:, 2, :], rs[:, 2, :], rs[:, 3, :], ALU.mult))
                for t in range(NT):
                    ins = dve.tensor_scalar(N[:, t, :], X[:, t, :], mv[:, t, 0:1], rs[:, 2, t:t + 1],
                                            ALU.subtract, ALU.mult)
                    if t % TB == TB - 1:
                        ins.then_inc(rows.sem, 1)

            @block.scalar
            def _(act):
                act.preload_act_table(ACT.Sqrt)
                for n in range(2 if rms else 1):
                    act.wait_ge(variance.sem, variance.at(n + 1))
                    act.activation(rs[:, 1, :], rs[:, 0, :], ACT.Sqrt).then_inc(root.sem, 1)
                for b in range(B):
                    act.wait_ge(turned.sem, turned.at(b + 1))
                    act.activation(nT[:, b * L:(b + 1) * L], self.banks[b][:], ACT.Copy)

            @block.tensor
            def _(pe):
                for b in range(B):
                    pe.wait_ge(rows.sem, rows.at(b + 1))
                    for j in range(TB):
                        last = pe.transpose(self.banks[b][:, j * P:(j + 1) * P], N[:, b * TB + j, :], self.ident[:])
                    last.then_inc(turned.sem, 1)
        step.passed(7 if rms else 3)
        variance.passed(2 if rms else 1)
        root.passed(2 if rms else 1)
        rows.passed(B)
        turned.passed(B)

    def ffn0(self):
        nc, a = self.nc, self.a
        wload = self.semaphore_of("ffn0_weights")
        first = wload.start == 0
        if first:
            self.f0w = self.sb("f0w", [P, 3, P])
            self.f0bias = self.sb("f0bias", [P, P])
            self.f0wt = self.sb("f0wt", [P, P])
            self.f0wc = self.sb("f0wc", [P, P])
            self.f0y = self.sb("f0y", [P, NT, P])

        def load_weights(sp):
            sp.dma_start(self.f0w[:], a["f0w"]).then_inc(wload.sem, 16)
            sp.dma_start(self.f0bias[:], a["f0bias"]).then_inc(wload.sem, 16)

        self.normalise(sync=load_weights if first else None)
        folded = self.semaphore_of("ffn0_folded")
        folds = self.semaphore_of("ffn0_folds")
        lin = self.semaphore_of("ffn0_linear")
        biased = self.semaphore_of("ffn0_biased")
        tanhed = self.semaphore_of("ffn0_tanh")
        w, banks, X, y = self.f0w, self.banks, self.X, self.f0y
        with nc.Block() as block:
            @block.tensor
            def _(pe):
                if first:
                    pe.wait_ge(wload.sem, 32)
                    pe.matmul(banks[4][:, 0:P], w[:, 1, :], w[:, 0, :], start=True, stop=True).then_inc(folded.sem, 1)
                    pe.wait_ge(folds.sem, 1)
                    pe.matmul(banks[5][:, 0:P], self.f0wt[:], w[:, 2, :], start=True, stop=True).then_inc(folded.sem, 1)
                    pe.wait_ge(folds.sem, 2)
                for b in range(B):
                    for j in range(TB):
                        t = b * TB + j
                        last = pe.matmul(banks[b][:, j * P:(j + 1) * P], self.nT[:, t * P:(t + 1) * P],
                                         self.f0wc[:], start=True, stop=True)
                    last.then_inc(lin.sem, 1)

            @block.vector
            def _(dve):
                if first:
                    dve.wait_ge(folded.sem, 1)
                    dve.tensor_copy(self.f0wt[:], banks[4][:, 0:P]).then_inc(folds.sem, 1)
                    dve.wait_ge(folded.sem, 2)
                    dve.tensor_copy(self.f0wc[:], banks[5][:, 0:P]).then_inc(folds.sem, 1)
                for b in range(B):
                    dve.wait_ge(lin.sem, lin.at(b + 1))
                    dve.tensor_tensor(y[:, b * TB:(b + 1) * TB, :], banks[b][:].rearrange("p (t c) -> p t c", t=TB),
                                      self.f0bias[:].unsqueeze(1).broadcast_to([P, TB, P]),
                                      ALU.add).then_inc(biased.sem, 1)
                for b in range(B):
                    dve.wait_ge(tanhed.sem, tanhed.at(b + 1))
                    s = slice(b * TB, (b + 1) * TB)
                    dve.scalar_tensor_tensor(out=X[:, s, :], in0=y[:, s, :], scalar=0.5, in1=X[:, s, :],
                                             op0=ALU.mult, op1=ALU.add)

            @block.scalar
            def _(act):
                for b in range(B):
                    act.wait_ge(biased.sem, biased.at(b + 1))
                    s = slice(b * TB, (b + 1) * TB)
                    act.activation(y[:, s, :], y[:, s, :], ACT.Tanh).then_inc(tanhed.sem, 1)
        if first:
            wload.passed(32)
        for x in (lin, biased, tanhed):
            x.passed(B)

    def gla(self):
        nc, a, X, nT, banks, psum = self.nc, self.a, self.X, self.nT, self.banks, self.psum
        stage = ExitStack()

        def sb(name, shape, dt=F32):
            return self.sb(f"g_{name}", shape, dt, stage)

        W3 = 3 * C
        NG = 3 * NH0
        WA = sb("WA", [P, W3 + NG])
        NWC = sb("NWC", [P, 1])
        GB = sb("GB", [P, NG])
        WO = sb("WO", [P, C])
        BO = sb("BO", [P, C])
        COS = sb("COS", [P, TB * 2 * C])
        SIN = sb("SIN", [P, TB * 2 * C])
        UPTO = sb("UPTO", [P, P])
        AFTER = sb("AFTER", [P, P])
        FUT = sb("FUT", [P, L])
        FUTB = sb("FUTB", [P, L], BF16)
        HM = sb("HM", [P, NH0])
        BM = sb("BM", [P, P])
        ONES = sb("ONES", [P, P])
        MINUS = sb("MINUS", [P, P])
        Z = sb("Z", [P, 4, NT, NG])
        LS = sb("LS", [P, NT, NG])
        SG = sb("SG", [P, NT, 2 * NH0])
        EF = sb("EF", [P, NT, NH0])
        EE = sb("EE", [P, NT, NH0])
        EM = sb("EM", [P, NT, NH0])
        GV = sb("GV", [P, NT, NH0])
        GE = sb("GE", [P, NT, NH0])
        MD = sb("MD", [P, NT])
        HS = sb("HS", [P, 2, P])
        CU = sb("CU", [P, 2, NH0, P])
        T1 = sb("T1", [P, 2 * C])
        T2 = sb("T2", [P, 2 * C])
        QK = sb("QK", [P, B, 2 * C])
        QKT = sb("QKT", [P, 2, 2 * C])
        QX = sb("QX", [P, 2, NH0, P])
        VG = sb("VG", [P, B, C])
        VE = sb("VE", [P, B, C])
        D = sb("D", [P, B, NH0 * P])
        A = sb("A", [P, 2, NH0 * P])
        Y1 = sb("Y1", [P, C])
        Y2 = sb("Y2", [P, C])
        YO = sb("YO", [P, 2, C])
        YT = sb("YT", [P, 2, C])
        UM = sb("UM", [P, C])
        M = sb("M", [P, B, C])
        loaded = self.semaphore_of("gla_load")
        arrays = [(WA, "gla_w"), (NWC, "gla_nw"), (GB, "gla_gb"), (WO, "gla_wo"), (BO, "gla_bo"), (COS, "cos"),
                  (SIN, "sin"), (UPTO, "upto"), (AFTER, "after"), (FUT, "future"), (HM, "headmask"),
                  (BM, "blockmask")]

        def load(sp):
            for dst, name in arrays:
                sp.dma_start(dst[:], a[name]).then_inc(loaded.sem, 16)
            sp.wait_ge(loaded.sem, 16 * len(arrays))

        self.normalise(rms=True, sync=load)
        names = "weighted gates logs exps sums sumexp step".split()
        loop_names = ("tile cumul expand proj expo decay rot vv qkT qkTc "
                 "sim attn mixed yo state yT yTc outp x rope ystep").split()
        S = {n: self.semaphore_of(f"gla_{n}") for n in names + loop_names}

        with nc.Block() as block:
            @block.gpsimd
            def _(pool):
                for n in loop_names:
                    S[n].credit(pool)

            @block.tensor
            def _(pe):
                pe.wait_ge(S["weighted"].sem, 1)
                for t in range(NT):
                    last = pe.matmul(banks[0][:, t * NG:(t + 1) * NG], nT[:, t * P:(t + 1) * P], WA[:, W3:W3 + NG],
                                     start=True, stop=True)
                last.then_inc(S["gates"].sem, 1)
                pe.wait_ge(S["logs"].sem, 2)
                for n, m in enumerate((UPTO, AFTER, ONES)):
                    last = pe.matmul(banks[1 + n][:, 0:NT * NH0], m[:], LS[:, :, 0:NH0], start=True, stop=True)
                last.then_inc(S["sums"].sem, 1)

            @block.scalar
            def _(act):
                act.wait_ge(S["logs"].sem, 1)
                act.activation(Z[:, 3], Z[:, 1], ACT.Exp, scale=-1.0).then_inc(S["exps"].sem, 1)
                act.wait_ge(S["exps"].sem, 1)
                act.activation(Z[:, 3], Z[:, 3], ACT.Ln, bias=1.0).then_inc(S["exps"].sem, 1)
                act.wait_ge(S["logs"].sem, 2)
                act.activation(SG[:], LS[:, :, NH0:NG], ACT.Exp)
                act.wait_ge(S["sums"].sem, 1)
                for n, e in enumerate((EF, EE, EM)):
                    last = act.activation(e[:], banks[1 + n][:, 0:NT * NH0].rearrange("p (t h) -> p t h", h=NH0),
                                          ACT.Exp)
                last.then_inc(S["sumexp"].sem, 1)

            @block.vector
            def _(dve):
                ch = Chain(dve, S["step"])
                dve.memset(ONES[:], 1.0)
                dve.memset(MINUS[:], -1.0)
                dve.memset(M[:], 0.0)
                dve.tensor_copy(FUTB[:], FUT[:])
                dve.tensor_scalar(WA[:], WA[:], NWC[:, 0:1], None, ALU.mult).then_inc(S["weighted"].sem, 1)
                dve.tensor_tensor(X[:], X[:], BO[:].unsqueeze(1).broadcast_to([P, NT, C]), ALU.add)
                dve.wait_ge(S["gates"].sem, 1)
                z, az, neg = Z[:, 0], Z[:, 1], Z[:, 2]
                ch.link(dve.tensor_tensor(z, banks[0][:, 0:NT * NG].rearrange("p (t g) -> p t g", g=NG),
                                          GB[:].unsqueeze(1).broadcast_to([P, NT, NG]), ALU.add))
                ch.link(dve.tensor_scalar(neg, z, -1.0, None, ALU.mult))
                dve.tensor_tensor(az, z, neg, ALU.max).then_inc(S["logs"].sem, 1)
                ch.link(dve.tensor_scalar(neg, neg, 0.0, None, ALU.max))
                dve.wait_ge(S["exps"].sem, 2)
                dve.scalar_tensor_tensor(out=LS[:], in0=neg, scalar=-1.0, in1=Z[:, 3], op0=ALU.mult,
                                         op1=ALU.subtract).then_inc(S["logs"].sem, 1)
                dve.wait_ge(S["sumexp"].sem, 1)
                ch.link(dve.tensor_scalar(GV[:], SG[:, :, 0:NH0], DH0 ** -0.5, None, ALU.mult))
                dve.tensor_tensor(GE[:], GV[:], EE[:], ALU.mult)
                ch.link(dve.tensor_tensor(Z[:, 0, :, 0:NH0], EM[:], HM[:].unsqueeze(1).broadcast_to([P, NT, NH0]),
                                          ALU.mult))
                dve.tensor_reduce(MD[:], Z[:, 0, :, 0:NH0], AX, ALU.add)

        class Item:

            def __init__(self, c, b, off=0, first=False, last=False):
                k, self.b = (b + off) // B, (b + off) % B
                self.real = not (first and b + off < 0) and not (last and b + off >= B)
                self.n = c * B + (b + off)
                self.p = self.b % 2
                self.tile = c + (k + self.b * TB)
                self.column = c * P + (k * P + self.b * L)
                self.angles = c * (2 * C) + k * 2 * C

        def need(eng, name, it, done):
            if not (isinstance(it.n, int) and it.n + done <= 0):
                eng.wait_ge(S[name].sem, it.n + S[name].at(done))

        def drive(eng, step):
            for b in range(B):
                step(0, b, True, False)
            with eng.Fori(1, TB - 1) as c:
                for b in range(B):
                    step(c, b, False, False)
            for b in range(B):
                step(TB - 1, b, False, True)

        def per_head(ap, it, w):
            return ap[:, bass.ds(it.tile, 1)].rearrange("p o h -> p (o h)").unsqueeze(2).broadcast_to([P, NH0, w])

        end = Item(TB - 1, B - 1)

        with nc.Block() as block:
            @block.gpsimd
            def _(pool):
                def stage_tile(it):
                    need(pool, "proj", it, -1)
                    pool.tensor_copy(HS[:, it.p, :], nT[:, bass.ds(it.column, P)]).then_inc(S["tile"].sem, 1)
                    need(pool, "expo", it, -1)
                    pool.tensor_tensor(CU[:, it.p], UPTO[:].unsqueeze(1).broadcast_to([P, NH0, P]),
                                       per_head(LS[:, :, 0:NH0], it, P), ALU.mult).then_inc(S["cumul"].sem, 1)

                def spread(it):
                    need(pool, "qkTc", it, 1)
                    pool.tensor_tensor(QX[:, it.p], QKT[:, it.p, 0:P].unsqueeze(1).broadcast_to([P, NH0, P]),
                                       HM[:].unsqueeze(2).broadcast_to([P, NH0, P]), ALU.mult
                                       ).then_inc(S["expand"].sem, 1)

                def step(c, b, first, last):
                    nxt, new = (Item(c, b, off, first, last) for off in (1, 3))
                    if new.real:
                        stage_tile(new)
                    if nxt.real:
                        spread(nxt)
                for b in range(3):
                    stage_tile(Item(0, b))
                spread(Item(0, 0))
                drive(pool, step)

            @block.tensor
            def _(pe):
                def early(it):
                    need(pe, "tile", it, 1)
                    need(pe, "vv", it, 0)
                    pe.matmul(banks[0][:, 0:W3], HS[:, it.p, :], WA[:, 0:W3], start=True, stop=True
                              ).then_inc(S["proj"].sem, 1)
                    need(pe, "cumul", it, 1)
                    need(pe, "decay", it, 0)
                    for s in range(2):
                        h4 = CU[:, it.p, 4 * s:4 * s + 4, :].rearrange("p h t -> p (h t)")
                        pe.matmul(banks[1 + s], ONES[:], h4, start=True, stop=False)
                        for h in range(4):
                            pe.matmul(banks[1 + s][:, h * P:(h + 1) * P], CU[:, it.p, 4 * s + h, :], MINUS[:],
                                      start=False, stop=False)
                        last = pe.matmul(banks[1 + s], self.identb[:], FUTB[:], start=False, stop=True)
                    last.then_inc(S["expo"].sem, 1)

                def turn(it):
                    need(pe, "rot", it, 1)
                    need(pe, "qkTc", it, 0)
                    for s in range(2):
                        last = pe.transpose(banks[3][:, s * P:(s + 1) * P], QK[:, it.b, s * P:(s + 1) * P], self.ident[:])
                    last.then_inc(S["qkT"].sem, 1)

                def sim(it):
                    need(pe, "expand", it, 1)
                    need(pe, "attn", it, 0)
                    for s in range(2):
                        last = pe.matmul(banks[4 + s], QKT[:, it.p, P:2 * P],
                                         QX[:, it.p, 4 * s:4 * s + 4, :].rearrange("p h t -> p (h t)"),
                                         start=True, stop=True)
                    last.then_inc(S["sim"].sem, 1)

                def mixed(it):
                    need(pe, "state", it, 0)
                    pe.matmul(banks[6][:, 2 * C:3 * C], QK[:, it.b, C:2 * C], VE[:, it.b, :], start=True, stop=True)
                    pe.matmul(banks[6][:, C:2 * C], QKT[:, it.p, 0:P], M[:, it.b, :], start=True, stop=True)
                    need(pe, "attn", it, 1)
                    for h in range(NH0):
                        s = slice(h * DH0, (h + 1) * DH0)
                        last = pe.matmul(banks[6][:, s], A[:, it.p, h * P:(h + 1) * P], VG[:, it.b, s],
                                         start=True, stop=True)
                    last.then_inc(S["mixed"].sem, 1)

                def turn_out(it):
                    need(pe, "yo", it, 1)
                    need(pe, "x", it, 0)
                    pe.transpose(banks[7][:, P:2 * P], YO[:, it.p, :], self.ident[:]).then_inc(S["yT"].sem, 1)

                def out(it):
                    need(pe, "yTc", it, 1)
                    pe.matmul(banks[7][:, 0:C], YT[:, it.p, :], WO[:], start=True, stop=True).then_inc(S["outp"].sem, 1)

                def step(c, b, first, last):
                    old, now, nxt, new = (Item(c, b, off, first, last) for off in (-1, 0, 1, 2))
                    sim(now)
                    if old.real:
                        turn_out(old)
                    if nxt.real:
                        turn(nxt)
                    if new.real:
                        early(new)
                    if old.real:
                        out(old)
                    mixed(now)
                early(Item(0, 0))
                early(Item(0, 1))
                turn(Item(0, 0))
                drive(pe, step)
                turn_out(end)
                out(end)

            @block.scalar
            def _(act):
                act.preload_act_table(ACT.Exp)

                def decay(it):
                    need(act, "expo", it, 1)
                    need(act, "attn", it, -3)
                    act.activation(D[:, it.b, :], psum[:, 1:3, :].rearrange("p a n -> p (a n)"), ACT.Exp
                                   ).then_inc(S["decay"].sem, 1)

                def take_qk(it):
                    need(act, "qkT", it, 1)
                    act.activation(QKT[:, it.p, :], banks[3][:, 0:2 * P], ACT.Copy).then_inc(S["qkTc"].sem, 1)

                def take_y(it):
                    need(act, "yT", it, 1)
                    act.activation(YT[:, it.p, :], banks[7][:, P:2 * P], ACT.Copy).then_inc(S["yTc"].sem, 1)

                def step(c, b, first, last):
                    old, nxt, new = (Item(c, b, off, first, last) for off in (-1, 1, 2))
                    if old.real:
                        take_y(old)
                    if nxt.real:
                        take_qk(nxt)
                    if new.real:
                        decay(new)
                decay(Item(0, 0))
                decay(Item(0, 1))
                take_qk(Item(0, 0))
                drive(act, step)
                take_y(end)

            @block.vector
            def _(dve):
                def early(it):
                    need(dve, "proj", it, 1)
                    need(dve, "rot", it, 0)
                    qk = banks[0][:, 0:2 * C].rearrange("p (g i d) -> p g i d", i=2, d=DH0 // 2)
                    t2 = T2[:].rearrange("p (g i d) -> p g i d", i=2, d=DH0 // 2)
                    angles = bass.ds(it.angles, 2 * C)
                    sin = SIN[:, angles].rearrange("p (g i d) -> p g i d", i=2, d=DH0 // 2)
                    dve.tensor_tensor(T1[:], banks[0][:, 0:2 * C], COS[:, angles], ALU.mult)
                    dve.tensor_tensor(t2[:, :, 0, :], qk[:, :, 1, :], sin[:, :, 0, :], ALU.mult)
                    dve.tensor_tensor(t2[:, :, 1, :], qk[:, :, 0, :], sin[:, :, 1, :], ALU.mult
                                      ).then_inc(S["rope"].sem, 1)
                    v = banks[0][:, 2 * C:W3].rearrange("p (h d) -> p h d", h=NH0)
                    dve.tensor_tensor(VG[:, it.b].rearrange("p (h d) -> p h d", h=NH0), v, per_head(GV, it, DH0),
                                      ALU.mult)
                    dve.tensor_tensor(VE[:, it.b].rearrange("p (h d) -> p h d", h=NH0), v, per_head(GE, it, DH0),
                                      ALU.mult).then_inc(S["vv"].sem, 1)
                    need(dve, "rope", it, 1)
                    dve.tensor_tensor(QK[:, it.b, :], T1[:], T2[:], ALU.add).then_inc(S["rot"].sem, 1)

                def decayed(it):
                    need(dve, "sim", it, 1)
                    need(dve, "decay", it, 1)
                    dve.tensor_tensor(A[:, it.p, :], psum[:, 4:6, :].rearrange("p a n -> p (a n)"), D[:, it.b, :],
                                      ALU.mult).then_inc(S["attn"].sem, 1)

                def gated(it):
                    need(dve, "mixed", it, 1)
                    need(dve, "state", it, 0)
                    need(dve, "yo", it, 0)
                    ch = Chain(dve, S["ystep"], it.n * 2)
                    y1, y2 = Y1[:].rearrange("p (h d) -> p h d", h=NH0), Y2[:].rearrange("p (h d) -> p h d", h=NH0)
                    dve.tensor_tensor(UM[:], banks[6][:, 2 * C:3 * C], BM[:], ALU.mult)
                    ch.link(dve.tensor_tensor(y1, banks[6][:, C:2 * C].rearrange("p (h d) -> p h d", h=NH0),
                                              per_head(EF, it, DH0), ALU.mult))
                    ch.link(dve.tensor_tensor(Y2[:], banks[6][:, 0:C], Y1[:], ALU.add))
                    dve.tensor_tensor(YO[:, it.p].rearrange("p (h d) -> p h d", h=NH0), y2,
                                      per_head(SG[:, :, NH0:2 * NH0], it, DH0), ALU.mult).then_inc(S["yo"].sem, 1)
                    dve.scalar_tensor_tensor(out=M[:, it.b, :], in0=M[:, it.b, :], scalar=MD[:, bass.ds(it.tile, 1)],
                                             in1=UM[:], op0=ALU.mult, op1=ALU.add).then_inc(S["state"].sem, 1)

                def residual(it):
                    need(dve, "outp", it, 1)
                    xt = X[:, bass.ds(it.tile, 1)].rearrange("p o c -> p (o c)")
                    dve.tensor_tensor(xt, banks[7][:, 0:C], xt, ALU.add).then_inc(S["x"].sem, 1)

                def step(c, b, first, last):
                    old, now, new = (Item(c, b, off, first, last) for off in (-1, 0, 2))
                    if old.real:
                        gated(old)
                    decayed(now)
                    if new.real:
                        early(new)
                    if old.real:
                        residual(old)
                early(Item(0, 0))
                early(Item(0, 1))
                drive(dve, step)
                gated(end)
                residual(end)
        stage.close()

    def route(self, kind, weights, bias, counted):
        nc, nT, rt, cw = self.nc, self.nT, self.rt, self.cw
        scored = self.semaphore_of("route_scored")
        step = self.semaphore_of("route_step")
        shifted = self.semaphore_of("route_shifted")
        powered = self.semaphore_of("route_powered")
        steps_seen = []
        s3 = [P, NT, E]

        def over(col):
            return col.unsqueeze(2).broadcast_to(s3)

        with nc.Block() as block:
            @block.gpsimd
            def _(pool):
                for s in counted:
                    if not s.start:
                        s.credit(pool)

            @block.tensor
            def _(pe):
                for t in range(NT):
                    last = pe.matmul(self.banks[0][:, t * E:(t + 1) * E], nT[:, t * P:(t + 1) * P], weights,
                                     start=True, stop=True)
                last.then_inc(scored.sem, 1)

            @block.scalar
            def _(act):
                if kind != 1:
                    act.preload_act_table(ACT.Exp)
                    act.wait_ge(shifted.sem, shifted.at(1))
                    act.activation(rt[:, 1], rt[:, 0], ACT.Exp).then_inc(powered.sem, 1)

            @block.vector
            def _(dve):
                ch = Chain(dve, step)
                logits = self.banks[0][:, 0:NT * E].rearrange("p (t e) -> p t e", e=E)
                v, e, best, tie, first = rt[:, 0], rt[:, 1], rt[:, 2], rt[:, 3], rt[:, 4]

                def best_of(values, into):
                    col = best[:, :, 0]
                    ch.link(dve.tensor_reduce(col, values, AX, ALU.max))
                    ch.link(dve.tensor_tensor(tie, values, over(col), ALU.is_equal))
                    ch.link(dve.tensor_tensor(tie, tie, self.prefer[:].unsqueeze(1).broadcast_to(s3), ALU.mult))
                    ch.link(dve.tensor_reduce(col, tie, AX, ALU.max))
                    ch.link(dve.tensor_tensor(into, tie, over(col), ALU.is_equal))

                dve.wait_ge(scored.sem, scored.at(1))
                if kind == 1:
                    ch.link(dve.tensor_tensor(v, logits, bias.unsqueeze(1).broadcast_to(s3), ALU.add))
                    best_of(v, first)
                    dve.tensor_scalar(cw[:], first, 0.5, None, ALU.mult)
                else:
                    ch.link(dve.tensor_reduce(best[:, :, 1], logits, AX, ALU.max))
                    dve.tensor_tensor(v, logits, over(best[:, :, 1]), ALU.subtract).then_inc(shifted.sem, 1)
                    dve.wait_ge(powered.sem, powered.at(1))
                    ch.link(dve.tensor_reduce(best[:, :, 1], e, AX, ALU.add))
                    ch.link(dve.reciprocal(best[:, :, 2], best[:, :, 1]))
                    ch.link(dve.tensor_tensor(e, e, over(best[:, :, 2]), ALU.mult))
                    best_of(e, first)
                    ch.link(dve.scalar_tensor_tensor(out=v, in0=first, scalar=-4.0, in1=e, op0=ALU.mult, op1=ALU.add))
                    best_of(v, rt[:, 5])
                    ch.link(dve.tensor_tensor(first, first, rt[:, 5], ALU.add))
                    if kind == 3:
                        dve.tensor_tensor(cw[:], first, e, ALU.mult)
                    else:
                        ch.link(dve.tensor_tensor(first, first, e, ALU.mult))
                        ch.link(dve.tensor_reduce(best[:, :, 3], first, AX, ALU.add))
                        ch.link(dve.tensor_scalar(best[:, :, 4], best[:, :, 3], 1e-9, 2.0, ALU.add, ALU.mult))
                        ch.link(dve.reciprocal(best[:, :, 5], best[:, :, 4]))
                        dve.tensor_tensor(cw[:], first, over(best[:, :, 5]), ALU.mult)
                steps_seen.append(ch.n)
        scored.passed(1)
        step.passed(steps_seen.pop())
        if kind != 1:
            shifted.passed(1)
            powered.passed(1)

    def moe(self, kind):
        nc, a, X, nT, cw, banks = self.nc, self.a, self.X, self.nT, self.cw, self.banks
        rload = self.semaphore_of("moe_small")
        if rload.start == 0:
            self.mw1 = self.sb("mw1", [P, 2, HI])
            self.mw2 = self.sb("mw2", [P, 2, IT, P])
            self.mh = self.sb("mh", [P, 2, IT, L])
            self.my = self.sb("my", [P, 2, TB, P])
            self.router = {kk: self.sb(f"router{kk}", [P, E]) for kk in (1, 2)}
            self.rbias = self.sb("rbias", [P, E])
            self.b1 = self.sb("b1", [P, E, IT])
            self.b1e = self.sb("b1e", [P, 2, IT])
            self.b2 = self.sb("b2", [P, E, P])
            self.game = self.sb("game", [P, E])
        small = rload.start == 0

        def load_small(sp):
            for dst, name in ((self.router[1], "router1"), (self.router[2], "router2"), (self.rbias, "rbias"),
                              (self.b1, "b1"), (self.b2, "b2"), (self.game, "game")):
                sp.dma_start(dst[:], a[name]).then_inc(rload.sem, 16)
            sp.wait_ge(rload.sem, 96)

        self.normalise(sync=load_small if small else None)
        if small:
            rload.passed(96)
        names = ["weights0", "weights1", "up", "gelu", "down", "gamed", "bias", "y", "step"]
        S = {n: self.semaphore_of(f"moe_{n}") for n in names}
        self.route(kind, self.router[kind][:], self.rbias[:] if kind == 1 else None, [S["y"]])
        w1, w2 = a[f"w1_{kind}"], a[f"w2_{kind}"]
        H, one = self.mh, kind == 1
        U = B

        def experts(eng, body):
            body(0, True, False)
            with eng.Fori(1, E // 2 - 1) as i:
                body(i, False, False)
            body(E // 2 - 1, False, True)

        with nc.Block() as block:
            @block.sync
            def _(sp):
                def expert(i, p, e):
                    sp.dma_start(self.mw1[:, p, :], w1[bass.ds(e, 1)].rearrange("e p n -> p (e n)")
                                 ).then_inc(S[f"weights{p}"].sem, 16)
                    sp.dma_start(self.mw2[:, p].rearrange("p a b -> p (a b)"),
                                 w2[bass.ds(e, 1)].rearrange("e p n -> p (e n)")).then_inc(S[f"weights{p}"].sem, 16)
                for p in range(2):
                    expert(0, p, p)
                with sp.Fori(1, E // 2) as i:
                    for p in range(2):
                        sp.wait_ge(S["down"].sem, i * 2 * U + S["down"].at((p - 1) * U))
                        expert(i, p, i * 2 + p)

            @block.tensor
            def _(pe):
                def up(i, p, u, first=False):
                    n = i * (2 * U) + (p * U + u)
                    if u == 0:
                        pe.wait_ge(S[f"weights{p % 2}"].sem, (i + p // 2) * 32 + S[f"weights{p % 2}"].at(32))
                    p %= 2
                    for it in range(IT):
                        if not first:
                            pe.wait_ge(S["gelu"].sem, n * IT + S["gelu"].at(it + 1 - IT))
                        pe.matmul(banks[it], self.mw1[:, p, it * P:(it + 1) * P], nT[:, u * L:(u + 1) * L],
                                  start=True, stop=True).then_inc(S["up"].sem, 1)

                def down(i, p, u, first):
                    n = i * (2 * U) + (p * U + u)
                    if not (first and p == 0 and u < 2):
                        pe.wait_ge(S["y"].sem, n + S["y"].at(-1))
                    for j in range(TB):
                        for it in range(IT):
                            if j == 0:
                                pe.wait_ge(S["gelu"].sem, n * IT + S["gelu"].at(it + 1))
                            last = pe.matmul(banks[4 + u % 2][:, j * P:(j + 1) * P], H[:, u % 2, it, j * P:(j + 1) * P],
                                             self.mw2[:, p, it, :], start=(it == 0), stop=(it == IT - 1))
                    last.then_inc(S["down"].sem, 1)

                def game(i, p):
                    pe.wait_ge(S[f"weights{p % 2}"].sem, (i + p // 2) * 32 + S[f"weights{p % 2}"].at(32))
                    if not (isinstance(i, int) and i + p == 0):
                        pe.wait_ge(S["bias"].sem, i * 2 + S["bias"].at(p))
                    for it in range(IT):
                        last = pe.matmul(banks[6][:, it:it + 1], self.mw1[:, p % 2, it * P:(it + 1) * P],
                                         self.game[:, bass.ds(i * 2 + p, 1)], start=True, stop=True)
                    last.then_inc(S["gamed"].sem, 1)

                def body(i, first, last):
                    for p in range(2):
                        final = last and p == 1
                        for u in range(U):
                            if u + 1 < U:
                                up(i, p, u + 1)
                            elif not final:
                                up(i, p + 1, 0)
                            if one and u == 2 and not final:
                                game(i, p + 1)
                            down(i, p, u, first)
                if one:
                    game(0, 0)
                up(0, 0, 0, True)
                experts(pe, body)

            @block.scalar
            def _(act):
                act.preload_act_table(ACT.Gelu)

                def body(i, first, last):
                    for p in range(2):
                        if one:
                            act.wait_ge(S["bias"].sem, i * 2 + S["bias"].at(p + 1))
                        for u in range(U):
                            n = i * (2 * U) + (p * U + u)
                            if not (first and p == 0 and u < 2):
                                act.wait_ge(S["down"].sem, n + S["down"].at(-1))
                            for it in range(IT):
                                act.wait_ge(S["up"].sem, n * IT + S["up"].at(it + 1))
                                act.activation(H[:, u % 2, it, :], banks[it], ACT.Gelu,
                                               bias=self.b1e[:, p, it:it + 1] if one else 0.0
                                               ).then_inc(S["gelu"].sem, 1)
                experts(act, body)

            @block.vector
            def _(dve):
                def bias(i, p):
                    dve.wait_ge(S["gamed"].sem, i * 2 + S["gamed"].at(p + 1))
                    dve.scalar_tensor_tensor(
                        out=self.b1e[:, p % 2, :], in0=banks[6][:, 0:IT], scalar=0.1,
                        in1=self.b1[:, bass.ds(i * 2 + p, 1), :].rearrange("p e n -> p (e n)"),
                        op0=ALU.mult, op1=ALU.add).then_inc(S["bias"].sem, 1)

                def body(i, first, last):
                    ch = Chain(dve, S["step"], i * (2 * U))
                    for p in range(2):
                        e = i * 2 + p
                        for u in range(U):
                            n = i * (2 * U) + (p * U + u)
                            if one and u == 2 and not (last and p == 1):
                                bias(i, p + 1)
                            dve.wait_ge(S["down"].sem, n + S["down"].at(1))
                            y = banks[4 + u % 2].rearrange("p (t c) -> p t c", t=TB)
                            if one:
                                ch.link(dve.tensor_tensor(self.my[:, u % 2], y,
                                                          self.b2[:, bass.ds(e, 1), :].broadcast_to([P, TB, P]),
                                                          ALU.add))
                                y = self.my[:, u % 2]
                            for j in range(TB):
                                t = u * TB + j
                                ins = dve.scalar_tensor_tensor(
                                    out=X[:, t, :], in0=y[:, j, :], scalar=cw[:, t, bass.ds(e, 1)], in1=X[:, t, :],
                                    op0=ALU.mult, op1=ALU.add)
                            ins.then_inc(S["y"].sem, 1)
                if one:
                    bias(0, 0)
                experts(dve, body)
        for p in range(2):
            S[f"weights{p}"].passed(32 * E // 2)
        S["up"].passed(E * U * IT)
        S["gelu"].passed(E * U * IT)
        S["down"].passed(E * U)
        S["y"].passed(E * U)
        if one:
            S["gamed"].passed(E)
            S["bias"].passed(E)
            S["step"].passed(E * U)

    def ffn3(self):
        nc, a, X, nT, cw, banks = self.nc, self.a, self.X, self.nT, self.cw, self.banks
        rload = self.semaphore_of("f3_weights")
        small = rload.start == 0
        if small:
            self.f3w = self.sb("f3w", [P, 2, E * H3])
            self.f3d = self.sb("f3d", [P, IT, P])
            self.f3r = self.sb("f3r", [P, E])
            self.f3n = self.sb("f3n", [P, 2, P])
            self.f3z = self.sb("f3z", [P, 2, 2, E * H3])
            self.f3t = self.sb("f3t", [P, 2, E * H3])
            self.f3h = self.sb("f3h", [P, 2, E * H3])
            self.f3hT = self.sb("f3hT", [P, 2, E * H3])

        def load_small(sp):
            sp.dma_start(self.f3w[:], a["f3w"]).then_inc(rload.sem, 16)
            sp.dma_start(self.f3d[:], a["f3d"]).then_inc(rload.sem, 16)
            sp.dma_start(self.f3r[:], a["f3r"]).then_inc(rload.sem, 16)
            sp.wait_ge(rload.sem, 48)

        self.normalise(sync=load_small if small else None)
        if small:
            rload.passed(48)
        names = ["tile", "proj", "z", "tanh", "h", "turned", "hT", "out", "x", "step"]
        S = {n: self.semaphore_of(f"f3_{n}") for n in names}
        self.route(3, self.f3r[:], None, [S["proj"], S["z"], S["x"]])
        n_, z, th, h, hT = self.f3n, self.f3z, self.f3t, self.f3h, self.f3hT
        M = NT // 2

        def scores(t):
            return cw[:, bass.ds(t, 1), :].rearrange("p o e -> p (o e)").unsqueeze(2).broadcast_to([P, E, H3])

        def v(ap):
            return ap.rearrange("p (e n) -> p e n", e=E)

        def drive(eng, step):
            for s in range(2):
                step(s, s)
            with eng.Fori(1, M - 1) as i:
                for p in range(2):
                    step(i * 2 + p, p)
            for s in range(2):
                step(NT - 2 + s, s, last=s + 1)

        with nc.Block() as block:
            @block.gpsimd
            def _(pool):
                def stage_tile(t, p, first):
                    if not first:
                        pool.wait_ge(S["proj"].sem, t + S["proj"].at(-1))
                    pool.tensor_copy(n_[:, p, :], nT[:, bass.ds(t * P, P)]).then_inc(S["tile"].sem, 1)
                for t in range(2):
                    stage_tile(t, t, True)
                with pool.Fori(1, M) as i:
                    for p in range(2):
                        stage_tile(i * 2 + p, p, False)

            @block.tensor
            def _(pe):
                def project(t, p, first=False):
                    pe.wait_ge(S["tile"].sem, t + S["tile"].at(1))
                    if not first:
                        pe.wait_ge(S["z"].sem, t + S["z"].at(-1))
                    for s in range(2):
                        last = pe.matmul(banks[2 * p + s], n_[:, p, :], self.f3w[:, s, :], start=True, stop=True)
                    last.then_inc(S["proj"].sem, 1)

                def down(t, p, first=False):
                    pe.wait_ge(S["hT"].sem, t + S["hT"].at(1))
                    if not first:
                        pe.wait_ge(S["x"].sem, t + S["x"].at(-1))
                    for it in range(IT):
                        last = pe.matmul(banks[6 + p][:, 0:P], hT[:, p, it * P:(it + 1) * P], self.f3d[:, it, :],
                                         start=(it == 0), stop=(it == IT - 1))
                    last.then_inc(S["out"].sem, 1)

                def step(t, p, last=0):
                    if not last:
                        project(t + 2, p)
                    pe.wait_ge(S["h"].sem, t + S["h"].at(1))
                    for it in range(IT):
                        turn = pe.transpose(banks[4 + p][:, it * P:(it + 1) * P], h[:, p, it * P:(it + 1) * P],
                                            self.ident[:])
                    turn.then_inc(S["turned"].sem, 1)
                    if not (isinstance(t, int) and t == 0):
                        down(t - 1, 1 - p, isinstance(t, int) and t <= 2)
                for t in range(2):
                    project(t, t, True)
                drive(pe, step)
                down(NT - 1, 1)

            @block.scalar
            def _(act):
                act.preload_act_table(ACT.Tanh)

                def tanh(t, p):
                    act.wait_ge(S["z"].sem, t + S["z"].at(1))
                    act.activation(th[:, p, :], z[:, p, 0, :], ACT.Tanh, scale=0.5).then_inc(S["tanh"].sem, 1)

                def step(t, p, last=0):
                    if last < 2:
                        tanh(t + 1, 1 - p)
                    act.wait_ge(S["turned"].sem, t + S["turned"].at(1))
                    act.activation(hT[:, p, :], banks[4 + p], ACT.Copy).then_inc(S["hT"].sem, 1)
                tanh(0, 0)
                drive(act, step)

            @block.vector
            def _(dve):
                def hidden(t, p, first=False):
                    dve.wait_ge(S["proj"].sem, t + S["proj"].at(1))
                    if not first:
                        dve.wait_ge(S["h"].sem, t + S["h"].at(-1))
                    for s in range(2):
                        last = dve.tensor_tensor(v(z[:, p, s, :]), v(banks[2 * p + s]), scores(t), ALU.mult)
                    last.then_inc(S["z"].sem, 1)
                    dve.wait_ge(S["tanh"].sem, t + S["tanh"].at(1))
                    if not first:
                        dve.wait_ge(S["turned"].sem, t + S["turned"].at(-1))
                    ch = Chain(dve, S["step"], t)
                    ch.link(dve.scalar_tensor_tensor(out=th[:, p, :], in0=th[:, p, :], scalar=1.0, in1=z[:, p, 0, :],
                                                     op0=ALU.add, op1=ALU.mult))
                    dve.scalar_tensor_tensor(out=h[:, p, :], in0=th[:, p, :], scalar=0.25, in1=z[:, p, 1, :],
                                             op0=ALU.mult, op1=ALU.mult).then_inc(S["h"].sem, 1)

                def residual(t, p):
                    dve.wait_ge(S["out"].sem, t + S["out"].at(1))
                    xt = X[:, bass.ds(t, 1), :].rearrange("p o c -> p (o c)")
                    dve.tensor_tensor(xt, banks[6 + p][:, 0:P], xt, ALU.add).then_inc(S["x"].sem, 1)

                def step(t, p, last=0):
                    static = isinstance(t, int)
                    if last < 2:
                        hidden(t + 1, 1 - p, static and t == 0)
                    if not (static and t == 0):
                        residual(t - 1, 1 - p)
                hidden(0, 0, True)
                drive(dve, step)
                residual(NT - 1, 1)
        for x in S.values():
            x.passed(NT)

    def attention(self, kind):
        nc, a, X, N, nT, psum, banks = self.nc, self.a, self.X, self.N, self.nT, self.psum, self.banks
        width, dims = {1: (64, 8), 2: (32, 4), 3: (64, 8)}[kind]
        slots = P // width
        T = slots * TB
        GROUPS = 8
        GC = C // GROUPS
        heads_g = {1: 2, 2: 2, 3: 1}[kind]
        DV = C // (GROUPS * heads_g)
        peaks = kind != 1
        stage = ExitStack()

        def sb(name, shape, dt=F32):
            return self.sb(f"{name}_{kind}", shape, dt, stage)

        masks = sb("masks", [P, 4 + 2 * slots])
        wst = sb("wst", [P, 2, P])
        HIGH = sb("HIGH", [P, 2, L], BF16)
        REST = sb("REST", [P, 2, L])
        LOW = sb("LOW", [P, 2, L], BF16)
        KS = sb("KS", [P, L], BF16)
        QS = sb("QS", [P, B, L], BF16)
        KM = sb("KM", [P, B, slots, L], BF16)
        EX = sb("EX", [P, 2, slots, TB, L])
        aload = self.semaphore_of("at_load")
        aux = [(masks[:], f"masks{kind}")]
        if kind == 1:
            WL = sb("WL", [P, NH1 * P])
            aux.append((WL[:], "wl1"))
            OT = sb("OT", [P, 2, L])
            SUMS = sb("SUMS", [P, 2, slots, TB])
            INV = sb("INV", [P, 2, slots, TB])
        else:
            V = sb("V", [P, NT, C])
            ON = sb("ON", [P, NT, C])
            VST = sb("VST", [P, 2, TB, 2, 32])
            OT = sb("OT", [P, L])
            QM = sb("QM", [P, 2, L], BF16)
            MAXI = sb("MAXI", [P, 2, TB, slots])
            NM = sb("NM", [P, TB, P], BF16)
            INV = sb("INV", [P, TB, slots])
            TMP = sb("TMP", [P, TB * slots, DV])
            WV = sb("WV", [P, C])
            WO = sb("WO", [P, C])
            NW = sb("NW", [P, C])
            MIX = sb("MIX", [P, 4])
            aux += [(WV[:], f"wv{kind}"), (WO[:], f"wo{kind}"), (NW[:], f"nw{kind}")]
            if kind == 2:
                LAM = sb("LAM", [P, 4, 8])
                LSC = sb("LSC", [P, 2, 8])
                LD = sb("LD", [P, 2])
                aux.append((LAM[:].rearrange("p a b -> p (a b)"), "lam"))
                SEL = self.ident
            else:
                BO = sb("BO", [P, C])
                SEL = sb("SEL", [P, 2 * 32])
                aux += [(BO[:], "bo"), (SEL[:], "sel3"), (MIX[:, 0:1], "dw")]
        names = ("proj high rest low stack masked masked_act peak reduced negated placed shifted score exp value taken "
                 "gathered joined weights0 weights1 vstage step pstep vproj vready fixed").split()
        S = {n: self.semaphore_of(f"at_{n}") for n in names}

        def load(sp):
            for dst, name in aux:
                sp.dma_start(dst, a[name]).then_inc(aload.sem, 16)
            sp.wait_ge(aload.sem, aload.at(16 * len(aux)))

        self.normalise(sync=load)
        aload.passed(16 * len(aux))

        if kind != 1:
            with nc.Block() as block:
                @block.tensor
                def _(pe):
                    for b in range(B):
                        for j in range(TB):
                            t = b * TB + j
                            last = pe.matmul(banks[b][:, j * P:(j + 1) * P], nT[:, t * P:(t + 1) * P], WV[:],
                                             start=True, stop=True)
                        last.then_inc(S["vproj"].sem, 1)

                @block.scalar
                def _(act):
                    for b in range(B):
                        act.wait_ge(S["vproj"].sem, S["vproj"].at(b + 1))
                        act.activation(V[:, b * TB:(b + 1) * TB, :].rearrange("p t c -> p (t c)"), banks[b], ACT.Copy)
                    if kind == 2:
                        act.wait_ge(S["fixed"].sem, S["fixed"].at(1))
                        act.activation(LD[:], LD[:], ACT.Exp).then_inc(S["vready"].sem, 1)

                @block.vector
                def _(dve):
                    ch = Chain(dve, S["step"])
                    dve.memset(NM[:], 0.0)
                    dve.memset(VST[:], 0.0)
                    if kind == 2:
                        ch.link(dve.tensor_tensor(LSC[:], LAM[:, 0:2], LAM[:, 2:4], ALU.mult))
                        dve.tensor_reduce(LD[:], LSC[:], AX, ALU.add).then_inc(S["fixed"].sem, 1)
                        dve.wait_ge(S["vready"].sem, S["vready"].at(1))
                        ch.link(dve.tensor_tensor(MIX[:, 2:3], LD[:, 1:2], LD[:, 0:1], ALU.subtract))
                        ch.link(dve.tensor_scalar(MIX[:, 0:1], MIX[:, 2:3], -0.8, None, ALU.add))
                    else:
                        ch.link(dve.tensor_scalar(MIX[:, 1:2], MIX[:, 0:1], -1.0, 1.0, ALU.mult, ALU.add))
                        ch.link(dve.tensor_scalar(MIX[:, 0:1], MIX[:, 0:1], -1.0, None, ALU.mult))
                    ch.link(dve.memset(VST[:, :, :, :, DV:DV + 1], 1.0))
            S["vproj"].passed(B)
            if kind == 2:
                S["fixed"].passed(1)
                S["vready"].passed(1)
            S["step"].passed(4 if kind == 2 else 3)

        class Item:

            def __init__(self, G, b, off, first, last):
                self.real = not (first and b + off < 0) and not (last and b + off >= B)
                self.G, self.b = G + (b + off) // B, (b + off) % B
                self.p = self.b % 2
                self.first = first and b + off == 0
                self.first4 = first and b + off < B

            def count(self, name, per, done):
                v = self.G * (B * per) + (self.b * per + done + S[name].start)
                return v

        def drive(eng, step, before=None):
            if before:
                before()
            for b in range(B):
                step(0, b, True, False)
            with eng.Fori(1, GROUPS - 1) as G:
                for b in range(B):
                    step(G, b, False, False)
            for b in range(B):
                step(GROUPS - 1, b, False, True)

        SCORE_BANKS, PEAK_BANKS, VALUE_BANKS = (5, 6, 7), (1, 3, 4), (3, 4)
        AT_FIRST, AT_PLACE, AT_SECOND, AT_VALUE, AT_TAKE, AT_GATHER = {
            1: (2, 4, 6, (1, 2, 3, 5), 5, (7,)),
            2: (0, 5, 8, (2, 4, 6, 9), 9, (14,)),
            3: (0, 3, 4, (1, 2, 3, 5), 5, (7,))}[kind]

        AT_MASK, AT_MASK_ACT = ((7, 9, 11), 7) if kind == 2 else ((6, 7), None)

        PLACE = "place"
        RING = list(range(T))
        if peaks:
            RING.insert(AT_PLACE + 1, PLACE)

        def score_bank(entry):
            return banks[SCORE_BANKS[RING.index(entry) % 3]]

        def last_user(entry, order):
            i = order.index(entry)
            before = [k for k in range(len(order)) if k % 3 == i % 3]
            return (order[i - 3], False) if i >= 3 else (order[before[-1]], True)

        qmat = QM if peaks else None
        MASK_ACT = (3,) if kind == 2 else ()
        MASK_DVE = tuple(j for j in range(slots) if j not in MASK_ACT)

        def mask(eng, it, part=None):
            on_act = part is None
            mine = MASK_ACT if on_act else MASK_DVE
            part = mine if on_act else part
            if part[0] == mine[0]:
                eng.wait_ge(S["stack"].sem, it.count("stack", 2, 1))
                if not it.first4:
                    eng.wait_ge(S["score"].sem, it.count("score", T, -3 * T))
            for j in part:
                out, keep, ones = KM[:, it.b, j, :], masks[:, 4 + j:5 + j], masks[:, 4 + slots + j:5 + slots + j]
                if on_act:
                    ins = eng.activation(out, KS[:], ACT.Identity, scale=keep, bias=ones)
                else:
                    ins = eng.tensor_scalar(out, KS[:], keep, ones, ALU.mult, ALU.add)
            if part[-1] == mine[-1]:
                ins.then_inc(S["masked_act" if on_act else "masked"].sem, 1)

        with nc.Block() as block:
            @block.sync
            def _(sp):
                def weights(G, first):
                    for s in range(2):
                        if not first:
                            sp.wait_ge(S["proj"].sem, Item(G, 0, 0, first, False).count("proj", 2, s - 1))
                        sp.dma_start(wst[:, s, :], a[f"ws{kind}"][G, :, (1 - s) * P:(2 - s) * P]
                                     ).then_inc(S[f"weights{s}"].sem, 16)
                for G in range(GROUPS):
                    weights(G, G == 0)

            @block.gpsimd
            def _(pool):
                def parts(it):
                    for s in range(2):
                        pool.wait_ge(S["rest"].sem, it.count("rest", 2, s + 1))
                        pool.tensor_tensor(LOW[:, s, :], REST[:, s, :],
                                           masks[:, 3 - 2 * s:4 - 2 * s].broadcast_to([P, L]), ALU.mult
                                           ).then_inc(S["low"].sem, 1)
                        pool.wait_ge(S["low"].sem, it.count("low", 2, s + 1))
                        if s == 0 and not it.first:
                            pool.wait_ge(S["masked"].sem, it.count("masked", 1, 0))
                            if MASK_ACT:
                                pool.wait_ge(S["masked_act"].sem, it.count("masked_act", 1, 0))
                        dst = KS[:] if s == 0 else QS[:, it.b, :]
                        pool.tensor_tensor(dst, REST[:, s, :], LOW[:, s, :], ALU.subtract).then_inc(S["stack"].sem, 1)

                def values(it):
                    if not (it.first or (it.first_b1)):
                        pool.wait_ge(S["value"].sem, it.count("value", 1, -1))
                    src = V[:, it.b * TB:(it.b + 1) * TB, bass.ds(it.G * GC, GC)]
                    pool.tensor_copy(VST[:, it.p, :, 0:heads_g, 0:DV],
                                     src.rearrange("p t (h d) -> p t h d", h=heads_g)).then_inc(S["vstage"].sem, 1)

                def start():
                    for b in range(3):
                        parts(Item(0, b, 0, True, False))

                def step(G, b, first, last):
                    new = Item(G, b, 3, first, last)
                    if kind != 1:
                        it = Item(G, b, 0, first, last)
                        it.first_b1 = first and b <= 1
                        values(it)
                    if new.real:
                        if peaks and not new.first4:
                            pool.wait_ge(S["shifted"].sem, new.count("shifted", 1, -3))
                        if not peaks and not new.first4:
                            pool.wait_ge(S["score"].sem, new.count("score", T, -3 * T))
                        parts(new)
                drive(pool, step, start)

            @block.tensor
            def _(pe):
                def project(it, s):
                    if it.b == 0:
                        pe.wait_ge(S[f"weights{s}"].sem, it.G * 16 + S[f"weights{s}"].at(16))
                    if s == 1 or not it.first:
                        pe.wait_ge(S["rest"].sem, it.count("rest", 2, s))
                    pe.matmul(banks[0], wst[:, s, :], nT[:, it.b * L:(it.b + 1) * L],
                              start=True, stop=True).then_inc(S["proj"].sem, 1)

                def peak(it, i):
                    j, qt = divmod(i, TB)
                    if i == 0:
                        pe.wait_ge(S["masked"].sem, it.count("masked", 1, 1))
                        if MASK_ACT:
                            pe.wait_ge(S["masked_act"].sem, it.count("masked_act", 1, 1))
                        pe.wait_ge(S["stack"].sem, it.count("stack", 2, 2))
                    tile, before = last_user(i, list(range(T)))
                    if not (before and it.first):
                        pe.wait_ge(S["reduced"].sem, it.count("reduced", T, tile + 1 - (T if before else 0)))
                    pe.matmul(banks[PEAK_BANKS[i % 3]], QS[:, it.b, qt * P:(qt + 1) * P], KM[:, it.b, j, :],
                              start=True, stop=True).then_inc(S["peak"].sem, 1)

                def bank_free(entry, now, mid):
                    user, before = last_user(entry, RING)
                    if before and now.first:
                        return
                    if user != PLACE:
                        pe.wait_ge(S["exp"].sem, now.count("exp", T, user + 1 - (T if before else 0)))
                    elif before:
                        pe.wait_ge(S["shifted"].sem, now.count("shifted", 1, 1))
                    elif mid.real:
                        pe.wait_ge(S["shifted"].sem, mid.count("shifted", 1, 1))

                def place(it, now=None):
                    pe.wait_ge(S["negated"].sem, it.count("negated", 1, 1))
                    if now:
                        bank_free(PLACE, now, it)
                    for qt in range(TB):
                        last = pe.matmul(score_bank(PLACE)[:, qt * P:(qt + 1) * P], NM[:, qt, :], self.identb[:],
                                         start=True, stop=True)
                    last.then_inc(S["placed"].sem, 1)

                def score(it, i, mid):
                    j, kt = divmod(i, TB)
                    if i == 0:
                        ready = "shifted" if peaks else "masked"
                        pe.wait_ge(S[ready].sem, it.count(ready, 1, 1))
                        if not peaks:
                            pe.wait_ge(S["stack"].sem, it.count("stack", 2, 2))
                    bank_free(i, it, mid)
                    q = qmat[:, it.p, :] if peaks else QS[:, it.b, :]
                    pe.matmul(score_bank(i), KM[:, it.b, j, kt * P:(kt + 1) * P], q,
                              start=True, stop=True).then_inc(S["score"].sem, 1)

                def value(it, c):
                    if c == 0:
                        pe.wait_ge(S["exp"].sem, it.count("exp", T, T))
                    if kind == 1:
                        j, kt = divmod(c, TB)
                        if kt == 0 and not it.first:
                            pe.wait_ge(S["taken"].sem, it.count("taken", 2, j - 1))
                        ins = pe.matmul(banks[VALUE_BANKS[j]], N[:, it.b * TB + kt, :], EX[:, it.p, j, kt, :],
                                        start=(kt == 0), stop=(kt == TB - 1))
                        if kt == TB - 1:
                            ins.then_inc(S["value"].sem, 1)
                        return
                    if c == 0:
                        pe.wait_ge(S["vstage"].sem, it.count("vstage", 1, 1))
                        if not it.first:
                            pe.wait_ge(S["joined"].sem, it.count("joined", 1, 0))
                    if kind == 2:
                        for j in range(slots):
                            ins = pe.matmul(banks[2][32 * j:32 * j + 32, :], VST[:, it.p, c, j // 2, :],
                                            EX[:, it.p, j, c, :], start=(c == 0), stop=(c == TB - 1))
                    elif c % 2 == 1:
                        for kt in (c - 1, c):
                            for j in range(slots):
                                at = 32 * (j + 2 * (kt % 2))
                                ins = pe.matmul(banks[2][at:at + 32, :], VST[:, it.p, kt, 0, :],
                                                EX[:, it.p, j, kt, :], start=(kt < 2), stop=(kt >= 2))
                    if c == TB - 1:
                        ins.then_inc(S["value"].sem, 1)

                def gather(it, j=0):
                    if kind == 1:
                        pe.wait_ge(S["taken"].sem, it.count("taken", 2, j + 1))
                        if not it.first:
                            pe.wait_ge(S["joined"].sem, it.count("joined", 2, j - 1))
                        for qt in range(TB):
                            ins = pe.matmul(banks[1 + j][:, qt * P:(qt + 1) * P], OT[:, j, qt * P:(qt + 1) * P],
                                            WL[:, bass.ds((it.G * 2 + j) * P, P)], start=True, stop=True)
                    else:
                        pe.wait_ge(S["taken"].sem, it.count("taken", 1, 1))
                        n = SEL.shape[1]
                        for qt in range(TB):
                            ins = pe.matmul(banks[2][:, qt * n:(qt + 1) * n], OT[:, qt * P:(qt + 1) * P],
                                            SEL[:], start=True, stop=True)
                    ins.then_inc(S["gathered"].sem, 1)

                def start():
                    begin = [Item(0, b, 0, True, False) for b in range(3)]
                    for it in begin:
                        for s in range(2):
                            project(it, s)
                    if peaks:
                        for it in begin[:2]:
                            for i in range(T):
                                peak(it, i)
                            if it.first:
                                place(it)

                def step(G, b, first, last):
                    old, now, mid, nxt, new = (Item(G, b, o, first, last) for o in (-1, 0, 1, 2, 3))
                    for i in range(T):
                        if new.real and i == AT_FIRST:
                            project(new, 0)
                        if new.real and i == AT_SECOND:
                            project(new, 1)
                        score(now, i, mid)
                        if peaks and nxt.real:
                            peak(nxt, i)
                        if peaks and mid.real and i == AT_PLACE:
                            place(mid, now)
                        if old.real:
                            if kind == 1:
                                value(old, i)
                                if i == T - 1:
                                    gather(old, 0)
                                    gather(old, 1)
                            else:
                                if i in AT_VALUE:
                                    value(old, AT_VALUE.index(i))
                                if i == AT_GATHER[0]:
                                    gather(old)
                drive(pe, step, start)
                end = Item(GROUPS - 1, B - 1, 0, False, True)
                for c in range(T if kind == 1 else TB):
                    value(end, c)
                for j in range(2 if kind == 1 else 1):
                    gather(end, j)

            @block.scalar
            def _(act):
                act.preload_act_table(ACT.Exp)

                def high(it, s):
                    act.wait_ge(S["proj"].sem, it.count("proj", 2, s + 1))
                    act.activation(HIGH[:, s, :], banks[0], ACT.Copy).then_inc(S["high"].sem, 1)

                def exp(it, i):
                    j, kt = divmod(i, TB)
                    if i == 0 and not it.first and not it.second:
                        act.wait_ge(S["value"].sem, it.count("value", 2 if kind == 1 else 1, -2 if kind == 1 else -1))
                        if kind == 1:
                            act.wait_ge(S["fixed"].sem, it.count("fixed", 1, -1))
                    act.wait_ge(S["score"].sem, it.count("score", T, i + 1))
                    act.activation(EX[:, it.p, j, kt, :], score_bank(i), ACT.Exp, scale=SM_SCALE,
                                   accum_out=SUMS[:, it.p, j, kt:kt + 1] if kind == 1 else None
                                   ).then_inc(S["exp"].sem, 1)

                def take(it):
                    act.wait_ge(S["value"].sem, it.count("value", 1, 1))
                    if not it.first:
                        act.wait_ge(S["gathered"].sem, it.count("gathered", 1, 0))
                    act.activation(OT[:], banks[2], ACT.Copy).then_inc(S["taken"].sem, 1)

                def start():
                    for b in range(3):
                        for s in range(2):
                            high(Item(0, b, 0, True, False), s)
                        if MASK_ACT:
                            mask(act, Item(0, b, 0, True, False))

                def step(G, b, first, last):
                    old, now, new = (Item(G, b, o, first, last) for o in (-1, 0, 3))
                    now.second = first and b == 1
                    for i in range(T):
                        exp(now, i)
                        if new.real and i in (AT_FIRST, AT_SECOND):
                            high(new, int(i == AT_SECOND))
                        if kind != 1 and old.real and i == AT_TAKE:
                            take(old)
                        if MASK_ACT and i == AT_MASK_ACT and new.real:
                            mask(act, new)
                drive(act, step, start)
                if kind != 1:
                    take(Item(GROUPS - 1, B - 1, 0, False, True))

            @block.vector
            def _(dve):
                st, st2 = S["step"], S["pstep"]

                def rest(it, s):
                    dve.wait_ge(S["high"].sem, it.count("high", 2, s + 1))
                    if not it.first:
                        dve.wait_ge(S["stack"].sem, it.count("stack", 2, s - 1))
                    dve.scalar_tensor_tensor(out=REST[:, s, :], in0=HIGH[:, s, :], scalar=masks[:, 2 - 2 * s:3 - 2 * s],
                                             in1=banks[0], op0=ALU.mult, op1=ALU.add).then_inc(S["rest"].sem, 1)

                def reduce(it, i):
                    j, qt = divmod(i, TB)
                    dve.wait_ge(S["peak"].sem, it.count("peak", T, i + 1))
                    dve.tensor_reduce(MAXI[:, it.p, qt, j:j + 1], banks[PEAK_BANKS[i % 3]], AX, ALU.max
                                      ).then_inc(S["reduced"].sem, 1)

                def negate(it):
                    dve.wait_ge(S["reduced"].sem, it.count("reduced", T, T))
                    if not it.first:
                        dve.wait_ge(S["placed"].sem, it.count("placed", 1, 0))
                    nm = NM[:].rearrange("p t (s w) -> p t s w", s=slots)
                    hi, mid = nm[:, :, :, 6 * dims], nm[:, :, :, 6 * dims + 1]
                    dve.tensor_scalar(hi, MAXI[:, it.p], -1.0, None, ALU.mult).then_inc(st.sem, 1)
                    dve.wait_ge(st.sem, it.count("step", 1, 1))
                    dve.scalar_tensor_tensor(out=mid, in0=MAXI[:, it.p], scalar=-1.0, in1=hi, op0=ALU.mult,
                                             op1=ALU.subtract).then_inc(S["negated"].sem, 1)

                def shift(it):
                    dve.wait_ge(S["placed"].sem, it.count("placed", 1, 1))
                    dve.tensor_tensor(QM[:, it.p, :], score_bank(PLACE), QS[:, it.b, :], ALU.add).then_inc(S["shifted"].sem, 1)

                def take(it, j):
                    dve.wait_ge(S["value"].sem, it.count("value", 2, j + 1))
                    if not it.first:
                        dve.wait_ge(S["gathered"].sem, it.count("gathered", 2, j - 1))
                    dve.tensor_copy(OT[:, j, :], banks[VALUE_BANKS[j]]).then_inc(S["taken"].sem, 1)

                def invert(it):
                    dve.wait_ge(S["exp"].sem, it.count("exp", T, T))
                    dve.reciprocal(INV[:, it.p], SUMS[:, it.p]).then_inc(S["fixed"].sem, 1)

                def join1(it, j):
                    dve.wait_ge(S["gathered"].sem, it.count("gathered", 2, j + 1))
                    dve.wait_ge(S["fixed"].sem, it.count("fixed", 1, 1))
                    if j == 1:
                        dve.wait_ge(S["joined"].sem, it.count("joined", 2, 1))
                    for qt in range(TB):
                        t = it.b * TB + qt
                        ins = dve.scalar_tensor_tensor(out=X[:, t, :], in0=banks[1 + j][:, qt * P:(qt + 1) * P],
                                                       scalar=INV[:, it.p, j, qt:qt + 1], in1=X[:, t, :],
                                                       op0=ALU.mult, op1=ALU.add)
                    ins.then_inc(S["joined"].sem, 1)

                def join(it, part=range(4)):
                    n = SEL.shape[1] // slots if kind == 2 else 32
                    O = banks[2][:, 0:TB * slots * n].rearrange("p (t s w) -> p t s w", t=TB, s=slots)
                    odd = INV[:].rearrange("p t (h i) -> p t h i", i=2)[:, :, :, 1]
                    both = TMP[:].rearrange("p (t h i) d -> p t h i d", t=TB, i=2)
                    out = ON[:, it.b * TB:(it.b + 1) * TB, bass.ds(it.G * GC, GC)]
                    if 0 in part:
                        dve.wait_ge(S["gathered"].sem, it.count("gathered", 1, 1))
                        if not it.first:
                            dve.wait_ge(S["joined"].sem, it.count("joined", 1, 0))
                        dve.reciprocal(INV[:], O[:, :, :, DV]).then_inc(st2.sem, 1)
                    if 1 in part:
                        dve.wait_ge(st2.sem, it.count("pstep", 3, 1))
                        dve.tensor_scalar(odd, odd, MIX[:, 0:1], None, ALU.mult).then_inc(st2.sem, 1)
                    if 2 in part:
                        dve.wait_ge(st2.sem, it.count("pstep", 3, 2))
                        dve.tensor_tensor(TMP[:], O.rearrange("p t s w -> p (t s) w")[:, :, 0:DV],
                                          INV[:].rearrange("p t s -> p (t s)").unsqueeze(2)
                                          .broadcast_to([P, TB * slots, DV]), ALU.mult).then_inc(st2.sem, 1)
                    if 3 in part:
                        dve.wait_ge(st2.sem, it.count("pstep", 3, 3))
                        dve.tensor_tensor(out.rearrange("p t (h d) -> p t h d", h=heads_g), both[:, :, :, 0, :],
                                          both[:, :, :, 1, :], ALU.add).then_inc(S["joined"].sem, 1)

                def start():
                    begin = [Item(0, b, 0, True, False) for b in range(3)]
                    for it in begin:
                        for s in range(2):
                            rest(it, s)
                        mask(dve, it, MASK_DVE)
                    if peaks:
                        for it in begin[:2]:
                            for i in range(T):
                                reduce(it, i)
                            if it.first:
                                negate(it)
                                shift(it)

                def step(G, b, first, last):
                    old, now, mid, nxt, new = (Item(G, b, o, first, last) for o in (-1, 0, 1, 2, 3))
                    for i in range(T):
                        if peaks and nxt.real:
                            reduce(nxt, i)
                        if peaks and mid.real and i == 0:
                            negate(mid)
                        if peaks and i in AT_MASK and new.real:
                            mask(dve, new, [MASK_DVE[AT_MASK.index(i)]])
                        if peaks and i >= T - 2 and old.real:
                            join(old, [0] if i == T - 2 else [1])
                        if peaks and mid.real and i == AT_PLACE + 1:
                            shift(mid)
                        if new.real and i in (AT_FIRST + 1, AT_SECOND + 1):
                            rest(new, int(i == AT_SECOND + 1))
                        if kind == 1 and old.real:
                            if i == TB:
                                take(old, 0)
                    if kind == 1:
                        if old.real:
                            take(old, 1)
                            join1(old, 0)
                            join1(old, 1)
                        invert(now)
                        if new.real:
                            mask(dve, new, MASK_DVE)
                        return
                    if old.real:
                        join(old, [2, 3])
                drive(dve, step, start)
                end = Item(GROUPS - 1, B - 1, 0, False, True)
                if kind == 1:
                    for j in range(2):
                        take(end, j)
                    for j in range(2):
                        join1(end, j)
                else:
                    join(end)

        items = GROUPS * B
        for n in ("proj", "high", "rest", "low", "stack"):
            S[n].passed(2 * items)
        S["masked"].passed(items)
        if MASK_ACT:
            S["masked_act"].passed(items)
        for s in range(2):
            S[f"weights{s}"].passed(16 * GROUPS)
        S["score"].passed(T * items)
        S["exp"].passed(T * items)
        two = 2 if kind == 1 else 1
        for n in ("value", "taken", "gathered", "joined"):
            S[n].passed(two * items)
        if kind == 1:
            S["fixed"].passed(items)
        else:
            for n in ("peak", "reduced"):
                S[n].passed(T * items)
            for n in ("negated", "placed", "shifted", "vstage", "step"):
                S[n].passed(items)
            S["pstep"].passed(3 * items)
            self.attention_out(kind, S, ON, NW, WO, MIX, BO if kind == 3 else None, EX)
        stage.close()

    def attention1(self):
        self.attention(1)

    def attention_out(self, kind, S, ON, NW, WO, MIX, BO, EX):
        nc, X, banks = self.nc, self.X, self.banks
        step, sqrt_in, sqrt_out = S["step"], S["negated"], S["placed"]
        ready, proj, turned, taken = S["shifted"], S["gathered"], S["value"], S["taken"]
        flat = EX[:].rearrange("p a s t l -> p (a s t l)")
        SQ = flat[:, 0:NT * C].rearrange("p (t c) -> p t c", t=NT)
        ONT = flat[:, NT * C:2 * NT * C]
        G = 16 if kind == 2 else 1
        W = C // G
        RM = flat[:, 2 * NT * C:2 * NT * C + 3 * NT * 16].rearrange("p (a n) -> p a n", a=3)[:, :, 0:NT * G]
        eps = 1e-6 if kind == 2 else float(np.finfo(np.float32).eps)
        with nc.Block() as block:
            @block.vector
            def _(dve):
                ch = Chain(dve, step)
                on = ON[:].rearrange("p t c -> p (t c)")
                grouped = ON[:].rearrange("p t (g w) -> p (t g) w", g=G)
                ch.link(dve.tensor_tensor(SQ, ON[:], ON[:], ALU.mult))
                ch.link(dve.tensor_reduce(RM[:, 0, :], SQ.rearrange("p t (g w) -> p (t g) w", g=G), AX, ALU.add))
                dve.tensor_scalar(RM[:, 1, :], RM[:, 0, :], 1.0 / W, eps, ALU.mult, ALU.add).then_inc(sqrt_in.sem, 1)
                dve.wait_ge(sqrt_out.sem, sqrt_out.at(1))
                ch.link(dve.reciprocal(RM[:, 1, :], RM[:, 2, :]))
                ch.link(dve.tensor_tensor(grouped, grouped, RM[:, 1, :].unsqueeze(2).broadcast_to([P, NT * G, W]),
                                          ALU.mult))
                if kind == 2:
                    for b in range(B):
                        for t in range(TB):
                            ins = dve.scalar_tensor_tensor(
                                out=ONT[:, b * L:(b + 1) * L].rearrange("p (d h t) -> p t h d", d=8, t=TB)[:, t],
                                in0=ON[:, b * TB + t, :].rearrange("p (h d) -> p h d", d=8), scalar=0.2,
                                in1=NW[:].rearrange("p (h d) -> p h d", d=8), op0=ALU.mult, op1=ALU.mult)
                        ins.then_inc(ready.sem, 1)
                else:
                    for b in range(B):
                        s = slice(b * TB, (b + 1) * TB)
                        dve.tensor_tensor(ON[:, s, :], ON[:, s, :], NW[:].unsqueeze(1).broadcast_to([P, TB, C]),
                                          ALU.mult).then_inc(ready.sem, 1)
                for b in range(B):
                    dve.wait_ge(proj.sem, proj.at(b + 1))
                    s = slice(b * TB, (b + 1) * TB)
                    y = banks[4 + b].rearrange("p (t c) -> p t c", t=TB)
                    if kind == 3:
                        ch.link(dve.tensor_tensor(SQ[:, s, :], y, BO[:].unsqueeze(1).broadcast_to([P, TB, C]), ALU.add))
                        dve.scalar_tensor_tensor(out=X[:, s, :], in0=SQ[:, s, :], scalar=MIX[:, 1:2], in1=X[:, s, :],
                                                 op0=ALU.mult, op1=ALU.add)
                    else:
                        dve.tensor_tensor(X[:, s, :], y, X[:, s, :], ALU.add)

            @block.scalar
            def _(act):
                act.wait_ge(sqrt_in.sem, sqrt_in.at(1))
                act.activation(RM[:, 2, :], RM[:, 1, :], ACT.Sqrt).then_inc(sqrt_out.sem, 1)
                if kind == 3:
                    for b in range(B):
                        act.wait_ge(turned.sem, turned.at(b + 1))
                        act.activation(ONT[:, b * L:(b + 1) * L], banks[b], ACT.Copy).then_inc(taken.sem, 1)

            @block.tensor
            def _(pe):
                if kind == 3:
                    for b in range(B):
                        pe.wait_ge(ready.sem, ready.at(b + 1))
                        for j in range(TB):
                            last = pe.transpose(banks[b][:, j * P:(j + 1) * P], ON[:, b * TB + j, :], self.ident[:])
                        last.then_inc(turned.sem, 1)
                for b in range(B):
                    src = taken if kind == 3 else ready
                    pe.wait_ge(src.sem, src.at(b + 1))
                    for j in range(TB):
                        last = pe.matmul(banks[4 + b][:, j * P:(j + 1) * P], ONT[:, b * L + j * P:b * L + (j + 1) * P],
                                         WO[:], start=True, stop=True)
                    last.then_inc(proj.sem, 1)
        step.passed(8 if kind == 3 else 4)
        sqrt_in.passed(1)
        sqrt_out.passed(1)
        ready.passed(B)
        proj.passed(B)
        if kind == 3:
            turned.passed(B)
            taken.passed(B)



def token_tiles(x):
    return np.ascontiguousarray(np.asarray(x).reshape(NT, P, C).transpose(1, 0, 2))


def everywhere(v):
    return np.ascontiguousarray(np.broadcast_to(np.asarray(v).reshape(1, -1), (P, np.asarray(v).size)))


def layout(i):
    i = {k: np.asarray(v) for k, v in i.items()}
    a = {"x": token_tiles(i["L0_attn_x"])}
    a |= constants()
    a["f0w"] = np.stack([i["L0_ffn_weight"].T, i["L0_ffn_aux_weight1"], i["L0_ffn_aux_weight2"]], axis=1)
    a["f0bias"] = everywhere(i["L0_ffn_bias"])
    a["router1"] = i["L1_ffn_router_w"]
    a["router2"] = i["L2_ffn_router_w"].T
    a["rbias"] = everywhere(i["L1_ffn_router_b"])
    a["b1"] = i["L1_ffn_b1"].reshape(E, IT, P).transpose(2, 0, 1)
    a["b2"] = everywhere(i["L1_ffn_b2"]).reshape(P, E, P)
    a["game"] = i["L1_ffn_game_emb"].T
    for n in (1, 2):
        a[f"w1_{n}"] = i[f"L{n}_ffn_w1"]
        a[f"w2_{n}"] = i[f"L{n}_ffn_w2"].reshape(E, IT, P, C).transpose(0, 2, 1, 3).reshape(E, P, IT * C)
    w1, w3 = (i[f"L3_ffn_{w}"].transpose(1, 0, 2).reshape(C, E * H3) for w in ("w1", "w3"))
    a["f3w"] = np.stack([w1, w3], axis=1)
    a["f3d"] = i["L3_ffn_w2"].reshape(IT, P, C).transpose(1, 0, 2)
    a["f3r"] = i["L3_ffn_gate_w"]
    eye = np.eye(C, dtype=np.float32)
    a["ws1"] = stack_weights(eye, eye, 64, 8)
    a["wl1"] = i["L1_attn_weight"].reshape(NH1, C, C).transpose(1, 0, 2).reshape(C, NH1 * C)
    qkv = i["L2_attn_w_qkv"]
    a["ws2"] = stack_weights(qkv[:, 0:C], qkv[:, C:2 * C], 32, 4)
    a["ws3"] = stack_weights(i["L3_attn_Wq"].T, i["L3_attn_Wk"].T, 64, 8)
    a["wv2"], a["wv3"] = qkv[:, 2 * C:], i["L3_attn_Wv"].T
    a["wo2"], a["wo3"] = i["L2_attn_wo"], i["L3_attn_Wo"].T
    a["nw2"], a["nw3"] = everywhere(i["L2_attn_norm_w"]), everywhere(i["L3_attn_norm_w"])
    a["lam"] = everywhere(np.concatenate([i[f"L2_attn_lambda_{n}"] for n in ("q1", "q2", "k1", "k2")]))
    a["bo"] = everywhere(i["L3_attn_bo"])
    a["dw"] = everywhere(i["L3_attn_diff_weight"])
    a["gla_w"] = np.concatenate([i[f"L0_attn_{n}"] for n in ("Wq", "Wk", "Wv", "Wbeta", "Wig", "Wog")]).T
    a["gla_nw"] = i["L0_attn_norm_w"].reshape(C, 1)
    a["gla_gb"] = everywhere(np.concatenate([i[f"L0_attn_{n}"] for n in ("bbeta", "big", "bog")]))
    a["gla_wo"], a["gla_bo"] = i["L0_attn_Wout"].T, everywhere(i["L0_attn_bout"])
    return {k: np.ascontiguousarray(v) for k, v in a.items()}



def kernel(**inputs):
    import concourse.bacc as bacc
    from concourse.bass_utils import run_bass_kernel_spmd

    nc = bacc.Bacc("TRN2", target_bir_lowering=False, num_devices=1)
    arrays = {f"in_{name}_dram": x for name, x in layout(inputs).items()}
    aps = {name[3:-5]: nc.dram_tensor(name, x.shape, mybir.dt.from_np(x.dtype), kind="ExternalInput").ap()
           for name, x in arrays.items()}
    out = nc.dram_tensor("out_0_dram", (P, NT, C), F32, kind="ExternalOutput").ap()
    build(nc, aps, out)
    r = run_bass_kernel_spmd(nc, [arrays], core_ids=[0])
    return np.ascontiguousarray(r.results[0]["out_0_dram"].transpose(1, 0, 2)).reshape(B, L, C)
```
